# Optimizing a Trainium2 kernel written in Bass

```python
import numpy as np
import jax
import jax.numpy as jnp

def _softmax(x, axis=-1):
    return jax.nn.softmax(x, axis=axis)

def _gelu(x):
    return jax.nn.gelu(x, approximate=True)

def _silu(x):
    return jax.nn.silu(x)

def _sigmoid(x):
    return jax.nn.sigmoid(x)

def _layernorm(x, axis=-1, eps=1e-05):
    m = jnp.mean(x, axis=axis, keepdims=True)
    v = jnp.var(x, axis=axis, keepdims=True)
    return (x - m) / jnp.sqrt(v + eps)

def _scatter_add(tgt, idx, src, axis=0):
    return tgt.at[idx].add(src)

def _segment_sum(src, seg, n):
    return jax.ops.segment_sum(src, seg, n)
kernel_name = 'mk_gps_d1_gnn_r8_b361db'

def setup_inputs(seed: int=0):
    np.random.seed(seed)
    _w = jnp.asarray

    def _rec_inputs():
        import jax
        import jax.numpy as jnp
        _gk = jax.random.key(seed)
        x = -0.0003713 + 1 * jax.random.normal(jax.random.fold_in(_gk, 1), (6250, 256), jnp.float32)
        src = jax.random.randint(jax.random.fold_in(_gk, 2), (100000,), 0, 6250, jnp.int32)
        dst = jax.random.randint(jax.random.fold_in(_gk, 3), (100000,), 0, 6250, jnp.int32)
        _o = jnp.argsort(dst, stable=True)
        src = src[_o]
        dst = dst[_o]
        edge_weight = -7.32377e-05 + 0.176746 * jax.random.normal(jax.random.fold_in(_gk, 12), (100000,), jnp.float32)
        return (x, src, dst, edge_weight)
    x, src, dst, edge_weight = _rec_inputs()

    def _L0_gnn_setup():
        import jax, jax.numpy as jnp
        import numpy as np
        N_NODES = 6250
        NNZ = 200000
        D_FEAT = 256
        key = jax.random.key(seed)
        k_x, k_v, k_r, k_c = jax.random.split(key, 4)
        x = jax.random.normal(k_x, (N_NODES, D_FEAT), dtype=jnp.float32)
        std = 1.0 / np.sqrt(NNZ / N_NODES)
        values = jax.random.normal(k_v, (NNZ,), dtype=jnp.float32) * std
        row = jax.random.randint(k_r, (NNZ,), 0, N_NODES, dtype=jnp.int64)
        col = jax.random.randint(k_c, (NNZ,), 0, N_NODES, dtype=jnp.int64)
        return {'x': x, 'values': values, 'row': row, 'col': col}
    _L0_gnn_all = _L0_gnn_setup()
    _L0_gnn_in = {k: v for k, v in _L0_gnn_all.items() if k in ()}
    del _L0_gnn_all

    def _L0_mix_setup():
        import jax, jax.numpy as jnp
        import numpy as np
        A, Bc, Cc = (0.5, 1.0, 1.0)
        H = 8
        EPS = 1e-12

        def _normalize(t):
            n = jnp.linalg.norm(t, axis=-1, keepdims=True)
            return t / jnp.maximum(n, EPS)
        key = jax.random.key(seed)
        ks = jax.random.split(key, 5)
        B, N, C = (8, 256, 256)
        D = C // H
        x = jax.random.normal(ks[0], (B, N, C), dtype=jnp.float32)
        Wqkv = jax.random.normal(ks[1], (3 * H * D, C), dtype=jnp.float32) * 0.02
        bqkv = jnp.zeros((3 * H * D,), dtype=jnp.float32)
        Wproj = jax.random.normal(ks[2], (C, H * D), dtype=jnp.float32) * 0.02
        bproj = jnp.zeros((C,), dtype=jnp.float32)
        temperature = jnp.ones((1, H, 1, 1), dtype=jnp.float32)
        return {'x': x, 'Wqkv': Wqkv, 'bqkv': bqkv, 'Wproj': Wproj, 'bproj': bproj, 'temperature': temperature}
    _L0_mix_all = _L0_mix_setup()
    _L0_mix_in = {k: v for k, v in _L0_mix_all.items() if k in ('Wqkv', 'bqkv', 'Wproj', 'bproj', 'temperature')}
    del _L0_mix_all

    def _L0_ffn_setup():
        import jax, jax.numpy as jnp
        import numpy as np
        B, S, H, F, E, K = (8, 512, 256, 512, 16, 2)
        EPS = 1e-05
        key = jax.random.key(seed)
        ks = jax.random.split(key, 9)
        sc = 0.02
        return {'x': jax.random.normal(ks[0], (B, S, H), dtype=jnp.float32), 'gate_w': jax.random.normal(ks[1], (H, E), dtype=jnp.float32) * sc, 'gate_b': jnp.zeros((E,), dtype=jnp.float32), 'w1': jax.random.normal(ks[2], (E, H, F), dtype=jnp.float32) * sc, 'b1': jnp.zeros((E, F), dtype=jnp.float32), 'w2': jax.random.normal(ks[3], (E, F, H), dtype=jnp.float32) * sc, 'b2': jnp.zeros((E, H), dtype=jnp.float32), 'gamma': jnp.ones((H,), dtype=jnp.float32), 'beta': jnp.zeros((H,), dtype=jnp.float32)}
    _L0_ffn_all = _L0_ffn_setup()
    _L0_ffn_in = {k: v for k, v in _L0_ffn_all.items() if k in ('gate_w', 'gate_b', 'w1', 'b1', 'w2', 'b2', 'gamma', 'beta')}
    del _L0_ffn_all
    return {'x': x, 'src': src, 'dst': dst, 'edge_weight': edge_weight, 'L0_mix_Wqkv': _L0_mix_in['Wqkv'], 'L0_mix_bqkv': _L0_mix_in['bqkv'], 'L0_mix_Wproj': _L0_mix_in['Wproj'], 'L0_mix_bproj': _L0_mix_in['bproj'], 'L0_mix_temperature': _L0_mix_in['temperature'], 'L0_ffn_gate_w': _L0_ffn_in['gate_w'], 'L0_ffn_gate_b': _L0_ffn_in['gate_b'], 'L0_ffn_w1': _L0_ffn_in['w1'], 'L0_ffn_b1': _L0_ffn_in['b1'], 'L0_ffn_w2': _L0_ffn_in['w2'], 'L0_ffn_b2': _L0_ffn_in['b2'], 'L0_ffn_gamma': _L0_ffn_in['gamma'], 'L0_ffn_beta': _L0_ffn_in['beta']}

def reference(x, src, dst, edge_weight, L0_mix_Wqkv, L0_mix_bqkv, L0_mix_Wproj, L0_mix_bproj, L0_mix_temperature, L0_ffn_gate_w, L0_ffn_gate_b, L0_ffn_w1, L0_ffn_b1, L0_ffn_w2, L0_ffn_b2, L0_ffn_gamma, L0_ffn_beta):
    import jax
    import jax.numpy as jnp

    def _L0_gnn_ref(x, values, row, col):
        import jax, jax.numpy as jnp
        import numpy as np
        N_NODES = 6250
        NNZ = 200000
        D_FEAT = 256
        msgs = values[:, None] * x[col]
        out = jax.ops.segment_sum(msgs, row, num_segments=N_NODES)
        return out

    def _L0_mix_ref(x, Wqkv, bqkv, Wproj, bproj, temperature):
        import jax, jax.numpy as jnp
        import numpy as np
        A, Bc, Cc = (0.5, 1.0, 1.0)
        H = 8
        EPS = 1e-12

        def _normalize(t):
            n = jnp.linalg.norm(t, axis=-1, keepdims=True)
            return t / jnp.maximum(n, EPS)
        B, N, C = x.shape
        D = C // H
        scale = float(D) ** 0.25
        qkv = (x @ Wqkv.T + bqkv).reshape(B, N, 3, H, D)
        qkv = jnp.transpose(qkv, (2, 0, 3, 1, 4))
        q, k, v = (qkv[0], qkv[1], qkv[2])
        q = q * scale
        v1 = jnp.concatenate([jnp.ones((B, H, N, 1), dtype=v.dtype), v], axis=-1)
        qn = _normalize(q) * (scale * temperature)
        kn = _normalize(k) * scale
        vN = v1 / N
        kv_mod = jnp.einsum('bhni,bhnj,bhne->bhije', kn, kn, vN)
        kv = jnp.einsum('bhnd,bhne->bhde', kn, vN)
        vsum = jnp.sum(vN, axis=-2)[:, :, None, :]
        y = A * jnp.einsum('bhni,bhnj,bhije->bhne', qn, qn, kv_mod) + scale ** 2 * Bc * jnp.einsum('bhnd,bhde->bhne', qn, kv) + scale ** 4 * Cc * vsum
        y_norm, y = (y[..., :1], y[..., 1:])
        y = y / y_norm
        out = jnp.transpose(y, (0, 2, 1, 3)).reshape(B, N, H * D)
        return out @ Wproj.T + bproj

    def _L0_ffn_ref(x, gate_w, gate_b, w1, b1, w2, b2, gamma, beta):
        import jax, jax.numpy as jnp
        import numpy as np
        B, S, H, F, E, K = (8, 512, 256, 512, 16, 2)
        EPS = 1e-05
        gate_logits = x @ gate_w + gate_b
        topk_vals, topk_idx = jax.lax.top_k(gate_logits, K)
        topk_w = jax.nn.softmax(topk_vals, axis=-1)
        h = jax.nn.relu(jnp.einsum('bsh,ehf->bsef', x, w1) + b1)
        expert_out = jnp.einsum('bsef,efh->bseh', h, w2) + b2
        sel = jnp.take_along_axis(expert_out, topk_idx[:, :, :, None], axis=2)
        moe = jnp.sum(topk_w[..., None] * sel, axis=2)
        y = x + moe
        mu = jnp.mean(y, axis=-1, keepdims=True)
        var = jnp.var(y, axis=-1, keepdims=True)
        return (y - mu) / jnp.sqrt(var + EPS) * gamma + beta
    xn = _layernorm(x, axis=-1)
    x = x + _L0_gnn_ref(xn, edge_weight, src, dst) + _L0_mix_ref(xn[None], L0_mix_Wqkv, L0_mix_bqkv, L0_mix_Wproj, L0_mix_bproj, L0_mix_temperature)[0]
    x = x + _L0_ffn_ref(_layernorm(x, axis=-1)[None], L0_ffn_gate_w, L0_ffn_gate_b, L0_ffn_w1, L0_ffn_b1, L0_ffn_w2, L0_ffn_b2, L0_ffn_gamma, L0_ffn_beta)[0]
    return x

_drawn_inputs = setup_inputs


def setup_inputs(seed=0):
    import zlib

    import numpy as np

    out = dict(_drawn_inputs(seed))
    spreads = {'L0_mix_bqkv': (0.0, 0.311),
     'L0_mix_bproj': (0.0, 0.1),
     'L0_mix_temperature': (1.0, 0.6),
     'L0_ffn_gate_b': (0.0, 0.1),
     'L0_ffn_b1': (0.0, 0.787),
     'L0_ffn_b2': (0.0, 0.1),
     'L0_ffn_gamma': (1.0, 0.2),
     'L0_ffn_beta': (0.0, 0.1)}
    factors = {'L0_mix_Wqkv': 27.416}
    for name, (base, spread) in spreads.items():
        noise = np.random.default_rng([zlib.crc32(name.encode()), seed]).standard_normal(out[name].shape)
        drawn = base * np.exp(spread * noise) if base else spread * noise
        out[name] = jnp.asarray(drawn.astype(out[name].dtype))
    for name, factor in factors.items():
        out[name] = (out[name] * factor).astype(out[name].dtype)
    return out
```

```python
from contextlib import ExitStack

import concourse.bass as bass
from concourse import mybir

ALU = mybir.AluOpType
ACT = mybir.ActivationFunctionType
AX = mybir.AxisListType
F32 = mybir.dt.float32
I32 = mybir.dt.int32
U32 = mybir.dt.uint32

P = 128
N = 6250
E = 100000
C = 256
H, D = 8, 32
X = 16
F = 512
FC = F // P
NT = 50
NP = NT * P
EB = 8
NB = 2 * NT
assert NT * P >= N and NB * EB * P >= E
DW = 48
VH = D + 1
KC = 4
NACC = 2
AR = NP + P
SCALE = float(D) ** 0.25
EPS_N = 1e-12
EPS_LN = 1e-5
U = 5
NU = NT // U
R = NP + P
FT = 116
FTL = FT + 4
assert FT >= (2 * NP + X * (P - 1)) // P
ZR = X * R + 20 * P


def program(nc, x, srcT, dstT, wT, wqkvT, bqkv, wprojT, bproj, temp, gate_w, gate_b, w1, b1T, w2, b2,
            gamma, beta, out):
    with ExitStack() as ctx:
        def sb(name, shape, dt=F32):
            return ctx.enter_context(nc.sbuf_tensor(name, shape, dt))

        def sem(name):
            return ctx.enter_context(nc.semaphore(name))

        def sems(name, n):
            return [sem(f"{name}{i}") for i in range(n)]

        ds = bass.ds

        def window(t, offset, dims):
            a = t
            return bass.AP(tensor=a.tensor, offset=a.offset + offset, ap=[list(a.ap[0])] + dims)

        xn_dram = nc.dram_tensor("xn_dram", [NP, C], F32).ap()
        acc_dram = [nc.dram_tensor(f"acc_dram{k}", [AR, C], F32).ap() for k in range(NACC)]
        z_dram = nc.dram_tensor("z_dram", [ZR, C], F32).ap()
        y_dram = nc.dram_tensor("y_dram", [FT * P, C], F32).ap()

        rows = sb("rows", [P, NT, C])
        ident = sb("ident", [P, P])
        upper = sb("upper", [P, P])
        ones = sb("ones", [P, P])
        eps = sb("eps", [P, 1])
        gw = sb("gw", [P, 2, X])
        gb_b = sb("gb_b", [P, X])
        b1c = sb("b1c", [P, X * FC])
        iota16 = sb("iota16", [P, X])
        base16 = sb("base16", [P, X])
        mv = sb("mv", [P, NT, 2])
        rstd = sb("rstd", [P, NT])
        nbias = sb("nbias", [P, NT])
        topv = sb("topv", [P, NT, 2])
        posT = sb("posT", [P, NT, 2])
        expT = sb("expT", [P, NT, 2])
        crun = sb("crun", [P, X])
        st = sb("st", [P, U, 6])
        mv5 = sb("mv5", [P, U, 2])
        std5 = sb("std5", [P, U])

        big = sb("big", [P, 2 * X * 1024])
        used = [0]

        def part(shape, dt=F32):
            n = 1
            for k in shape[1:]:
                n *= k
            a = big[:, used[0]:used[0] + n]
            used[0] += n
            if dt != F32:
                a = a.bitcast(dt)
            if len(shape) == 3:
                a = a.rearrange("p (a b) -> p a b", a=shape[1])
            if len(shape) == 4:
                a = a.rearrange("p (a b c) -> p a b c", a=shape[1], b=shape[2])
            return a

        srcI = part([P, NB + 1, EB], I32)
        dstI = part([P, NB + 1, EB], I32)
        wE = part([P, NB + 1, EB])
        wqkv = part([P, 2, 3 * C])
        wproj = part([P, 2, C])
        bqkv_b = part([P, 3 * C])
        bproj_b = part([P, C])
        lower = part([P, P])
        mask_l = part([P, 4, VH])
        mask_s = part([P, H, VH])
        half0 = part([P, 1])
        rscale = part([P, NT])
        temp_b = part([P, H])
        fac = part([P, 2 * H])
        ssc = part([P, 2 * H])
        dummy = part([P, 1])
        xst = [part([P, C]) for _ in range(2)]
        xT = [part([P, 2, P]) for _ in range(2)]
        qkvb = part([P, 3 * C])
        sq = part([P, 2 * C])
        ss = part([P, 2 * H])
        nrm = part([P, 2 * H])
        rn = part([P, 2 * H])
        kd = [part([P, H, DW]) for _ in range(2)]
        kc = [part([P, C]) for _ in range(2)]
        v1 = [part([P, H, VH]) for _ in range(2)]
        kk0 = used[0]
        kk = [part([P, H, 16, D]) for _ in range(2)]
        k16 = [part([P, P]) for _ in range(2)]
        zero = big[:, kk0:kk0 + 13 * C]
        m2 = part([P, H * KC, VH])
        m1 = part([P, 2, 4 * VH])
        m16 = part([P, H * VH])
        m0 = part([P, H * VH])
        srcb = [part([P, EB]) for _ in range(2)]
        wb = [part([P, EB]) for _ in range(2)]
        dstb = [sb(f"dstb{k}", [P, EB], I32) for k in range(2)]
        idxb = [sb(f"idxb{k}", [P, EB], I32) for k in range(2)]
        cnt = part([P, EB])
        dup = part([P, EB])
        ddd = part([P, EB])
        wd = [part([P, P]) for _ in range(EB)]
        junk = [part([P, P]) for _ in range(4)]
        qq = [part([P, 4, P]) for _ in range(3)]
        yb = part([P, H, VH])
        yr = part([P, H])
        on = [part([P, C]) for _ in range(2)]
        oT = [part([P, 2, P]) for _ in range(2)]
        xin = [part([P, C]) for _ in range(2)]
        pr = part([P, C])
        assert used[0] <= 2 * X * 1024
        gx = [part([P, C]) for k in range(EB)]
        msg = part([P, EB, C])
        assert used[0] <= 2 * X * 1024
        w1s = big[:, 0:X * 1024].rearrange("p (e c f) -> p e c f", e=X, c=2)
        w2s = big[:, X * 1024:2 * X * 1024].rearrange("p (e c f) -> p e c f", e=X, c=FC)

        mid = sb("mid", [P, 5120])
        accb = mid[:, 0:2 * U * C].rearrange("p (k u c) -> p k u c", k=2, u=U)
        zt5 = [mid[:, 2560 + 1280 * k:3840 + 1280 * k].rearrange("p (u c) -> p u c", u=U) for k in range(2)]
        zT = [sb(f"zT{k}", [P, 2, P]) for k in range(2)]
        lg = sb("lg", [P, U, X])
        m8 = sb("m8", [P, U, 8])
        i8 = sb("i8", [P, U, 8], U32)
        idf = sb("idf", [P, U, 2])
        ranks = sb("ranks", [P, 5, U * X])
        oh = [ranks[:, k, :].rearrange("p (u e) -> p u e", u=U) for k in range(2)]
        cc, rk, pk = (ranks[:, k, :].rearrange("p (u e) -> p u e", u=U) for k in (2, 3, 4))
        csum = sb("csum", [P, X])
        posf = sb("posf", [P, U, 2])
        idxz = [sb(f"idxz{k}", [P, U, 2], I32) for k in range(2)]
        zeros = mid[:, 4480:4480 + C]
        zt = [mid[:, 256 * k:256 * (k + 1)] for k in range(4)]
        b2t = [mid[:, 1024 + 256 * k:1280 + 256 * k] for k in range(4)]
        yo = [mid[:, 2048 + 256 * k:2304 + 256 * k] for k in range(4)]
        hs = [mid[:, 3072 + 512 * k:3584 + 512 * k] for k in range(2)]
        hT = [mid[:, 4096 + 512 * k:4608 + 512 * k].rearrange("p (c n) -> p c n", c=FC) for k in range(2)]
        cntR = sb("cntR", [P, X])
        ntl = lg[:, 0, :]
        endt = lg[:, 1, :]
        shift = lg[:, 2, :]
        cmpy = mid[:, 0:NT * 2 * X].rearrange("p (t e) -> p t e", e=X)
        cmpt = mid[0:1, 0:FTL * X].rearrange("p (t e) -> p t e", e=X)
        cmpm = mid[0:1, 2560:2560 + FTL * X].rearrange("p (t e) -> p t e", e=X)
        cmpc = mid[:, 0:X * NT].rearrange("p (e j) -> p e j", e=X)
        tau = mid[0:1, 1920:1920 + FTL]
        thr = mid[:, 2040:2040 + NT]
        etau = mid[0:1, 4736:4736 + FTL]
        stau = mid[0:1, 4856:4856 + FTL]
        rowf = mid[0:1, 4976:4976 + FTL]
        rowI = ranks[0:1, :, :].rearrange("p a b -> p (a b)")[:, 0:FTL].bitcast(I32)
        expI = ranks[0:1, :, :].rearrange("p a b -> p (a b)")[:, FTL:2 * FTL].bitcast(I32)
        tailI = sb("tailI", [1, X], I32)

        yg = [big[:, 2560 * k:2560 * (k + 1)].rearrange("p (k u c) -> p k u c", k=2, u=U) for k in range(2)]
        zc = [big[:, 5120 + 1280 * k:6400 + 1280 * k].rearrange("p (u c) -> p u c", u=U) for k in range(2)]
        fc = [big[:, 7680 + 1280 * k:8960 + 1280 * k].rearrange("p (u c) -> p u c", u=U) for k in range(2)]
        fn = big[:, 10240:11520].rearrange("p (u c) -> p u c", u=U)
        gamma_b = big[:, 11520:11776]
        beta_b = big[:, 11776:12032]
        mvc = big[:, 12032:12032 + 2 * U].rearrange("p (u o) -> p u o", u=U)
        rc = big[:, 12048:12048 + U]
        nc5 = big[:, 12056:12056 + U]

        bank = [ctx.enter_context(nc.psum_tensor(f"bank{k}", [P, 512], F32)) for k in range(4)]
        bqk = ctx.enter_context(nc.psum_tensor("bqk", [P, 1024], F32))
        b6 = ctx.enter_context(nc.psum_tensor("b6", [P, 512], F32))
        b7 = ctx.enter_context(nc.psum_tensor("b7", [P, 512], F32))
        ps_src = b6[:].rearrange("p (j e) -> p j e", j=4)
        ps_xT = bqk[:, 0:C]
        ps_msg = b7[:].rearrange("p (j c) -> p j c", j=2)

        def chunk_out(c):
            return bank[c // 15][:, (c % 15) * VH:(c % 15 + 1) * VH]

        W4 = 4 * VH
        sum_k = [bank[2][:, 66 + W4 * g:66 + W4 * (g + 1)] for g in range(2)]
        sum_v = [bank[2][:, 66 + 2 * W4:66 + 3 * W4], bank[3][:, 2 * W4:3 * W4]]
        sum_16 = [bank[3][:, W4 * g:W4 * (g + 1)] for g in range(2)]
        ps_y = bqk[:, 0:H * VH]
        ps_pr = bank[3][:, 0:C]
        ps_oT = bank[3][:, C:2 * C]
        ps_zT = [b6[:, 0:C], b7[:, 0:C]]
        ps_lg = [bank[0][:, 0:U * X], bank[3][:, 0:U * X]]
        ps_rk = bank[1][:, 0:U * X]
        ps_cnt = bank[2][:, 0:X]
        ps_h = [bank[0], bank[1]]
        ps_hT = [bank[2], bank[3]]
        ps_y2 = [bqk[:, 0:C], bqk[:, 512:512 + C]]

        s_const = sem("s_const")
        s_cload = sem("s_cload")
        s_zeroed = sem("s_zeroed")
        s_etab = sem("s_etab")
        s_zero = sem("s_zero")
        s_dve = sem("s_dve")
        s_act = sem("s_act")
        s_ask = sem("s_ask")
        s_xin = sems("s_xin", 2)
        s_xn = sem("s_xn")
        s_xnst = sem("s_xnst")
        s_prep = sem("s_prep")
        s_tr = sem("s_tr")
        s_d = sem("s_d")
        s_msg = sem("s_msg")
        s_evac = sem("s_evac")
        s_idx = sem("s_idx")
        s_gath = sems("s_gath", EB)
        s_scat = sems("s_scat", EB)
        s_xst = sem("s_xst")
        s_xTp = sem("s_xTp")
        s_xT = sem("s_xT")
        s_qkv = sem("s_qkv")
        s_bias = sem("s_bias")
        s_sq = sem("s_sq")
        s_v1 = sem("s_v1")
        s_kk = sem("s_kk")
        s_acc = sem("s_acc")
        s_mom = sem("s_mom")
        s_qd = sem("s_qd")
        s_qtr = sem("s_qtr")
        s_qn = sem("s_qn")
        s_qq = sem("s_qq")
        s_yi = sem("s_yi")
        s_on = sem("s_on")
        s_oTp = sem("s_oTp")
        s_oT = sem("s_oT")
        s_pr = sem("s_pr")
        s_x1 = sem("s_x1")
        s_xr = sems("s_xr", 2)
        s_w = sem("s_w")
        s_accl = sem("s_accl")
        s_bx = sem("s_bx")
        s_z = sem("s_z")
        s_zTp = sem("s_zTp")
        s_zT = sem("s_zT")
        s_lg = sem("s_lg")
        s_cc = sem("s_cc")
        s_rk = sem("s_rk")
        s_idxz = sem("s_idxz")
        s_zsc = sems("s_zsc", 2)
        s_cnt = sem("s_cnt")
        s_tab = sem("s_tab")
        s_tail = sem("s_tail")
        s_dz = sem("s_dz")
        s_gb = sem("s_gb")
        s_ztin = sems("s_ztin", 4)
        s_b2in = sems("s_b2in", 4)
        s_yst = sems("s_yst", 4)
        f_zT = sem("f_zT")
        f_zTe = sem("f_zTe")
        f_h = sem("f_h")
        f_hs = sem("f_hs")
        f_hT = sem("f_hT")
        f_hTe = sem("f_hTe")
        f_y = sem("f_y")
        f_yo = sem("f_yo")
        s_idxc = sem("s_idxc")
        s_yg = sems("s_yg", 2)
        s_zc = sem("s_zc")
        s_fn = sem("s_fn")
        s_fo = sem("s_fo")
        s_ost = sems("s_ost", 2)

        s_here = sem("s_here")

        NCONST = 21
        NCLOAD = 16 * 8
        QI = 9

        block = ctx.enter_context(nc.Block())

        @block.sync
        def _(sp):
            def load_x(i, k):
                u = 2 * i + k
                sp.dma_start(rows[:, ds(u * U, U), :],
                             x[ds(u * U * P, U * P), :].rearrange("(u p) c -> p u c", p=P)).then_inc(s_xin[k], 16)

            load_x(0, 0)
            load_x(0, 1)
            sp.dma_start(srcI[:], srcT.rearrange("p (b j) -> p b j", j=EB)).then_inc(s_etab, 16)
            sp.dma_start(dstI[:], dstT.rearrange("p (b j) -> p b j", j=EB)).then_inc(s_etab, 16)
            sp.dma_start(wE[:], wT.rearrange("p (b j) -> p b j", j=EB)).then_inc(s_etab, 16)
            sp.wait_ge(s_zero, 1)
            q = AR // P
            parts = [(0, 13), (13, 26), (26, 39), (39, q)]
            for j in range(EB):
                a, b = parts[j // 2]
                sp.dma_start(acc_dram[j % 2][a * P:b * P, :].rearrange("(p r) c -> p (r c)", p=P),
                             zero[:, 0:(b - a) * C]).then_inc(s_zeroed, 16)
            with sp.Fori(1, NU // 2) as i:
                for k in range(2):
                    sp.wait_ge(s_xin[k], 16 * i)
                    load_x(i, k)
            with sp.Fori(0, NU) as u:
                sp.wait_ge(s_xn, u + 1)
                sp.dma_start(xn_dram[ds(u * U * P, U * P), :].rearrange("(u p) c -> p u c", p=P),
                             rows[:, ds(u * U, U), :]).then_inc(s_xnst, 16)
            def load_xr(i, k):
                sp.dma_start(xin[k], x[ds((2 * i + k) * P, P), :]).then_inc(s_xr[k], 16)

            load_xr(0, 0)
            load_xr(0, 1)
            with sp.Fori(1, NT // 2) as i:
                for k in range(2):
                    sp.wait_ge(s_x1, 2 * i + k - 1)
                    load_xr(i, k)
            sp.wait_ge(s_x1, NT)
            sp.wait_ge(s_evac, 4 + 4 * NB)
            for j in range(EB):
                sp.wait_ge(s_scat[j], 16 * NB)
            def load_acc(u):
                for k in range(2):
                    sp.dma_start(accb[:, k], acc_dram[k][ds(u * U * P, U * P), :].rearrange("(u p) c -> p u c", p=P)
                                 ).then_inc(s_accl, 16)

            load_acc(0)
            for u in range(1, NU):
                if u <= 8:
                    e = 4 * ((u - 1) % 4)
                    if u <= 4:
                        sp.dma_start(w1s[:, e:e + 4], w1[e:e + 4].rearrange("e (c p) f -> p e c f", p=P)).then_inc(s_w, 16)
                    else:
                        sp.dma_start(w2s[:, e:e + 4], w2[e:e + 4].rearrange("e (c p) f -> p e c f", p=P)).then_inc(s_w, 16)
                sp.wait_ge(s_bx, u)
                load_acc(u)
            for k in range(2):
                sp.wait_ge(s_zsc[k], 160 * (NU // 2))
            sp.wait_ge(s_dz, 3)
            for r in range(20):
                sp.dma_start(z_dram[X * R + r * P:X * R + (r + 1) * P, :], zeros).then_inc(s_tail, 16)
            sp.wait_ge(s_tab, 1)
            with sp.Fori(0, X) as e:
                row = sp.value_load(tailI[0:1, ds(e, 1)], min_val=0, max_val=X * R - P)
                sp.dma_start(z_dram[ds(row, P), :], zeros).then_inc(s_tail, 16)
            sp.wait_ge(s_tail, 16 * (20 + X))

            def load_tile(t, k):
                row = sp.value_load(rowI[0:1, ds(t, 1)], min_val=0, max_val=ZR - P)
                ex = sp.value_load(expI[0:1, ds(t, 1)], min_val=0, max_val=X - 1)
                sp.dma_start(zt[k], z_dram[ds(row, P), :]).then_inc(s_ztin[k], 16)
                sp.dma_start(b2t[k], bass.AP(tensor=b2.tensor, offset=b2.offset + ex * C, ap=[[0, P], [1, C]])).then_inc(s_b2in[k], 16)

            for k in range(4):
                load_tile(k, k)
            with sp.Fori(0, FT // 4) as i:
                for k in range(4):
                    t = 4 * i + k
                    sp.wait_ge(f_yo, t + 3)
                    sp.dma_start(y_dram[ds(t * P, P), :], yo[k]).then_inc(s_yst[k], 16)
                    sp.wait_ge(f_zT, t + 1)
                    load_tile(t + 4, k)
            for k in range(4):
                sp.wait_ge(s_yst[k], 16 * (FT // 4))
                sp.wait_ge(s_ztin[k], 16 * (FT // 4 + 1))
                sp.wait_ge(s_b2in[k], 16 * (FT // 4 + 1))
            sp.dma_start(gamma_b, gamma.partition_broadcast(P)).then_inc(s_gb, 16)
            sp.dma_start(beta_b, beta.partition_broadcast(P)).then_inc(s_gb, 16)
            sp.sem_inc(s_tail, 1)
            with sp.Fori(0, NU // 2) as i:
                for k in range(2):
                    u = 2 * i + k
                    sp.wait_ge(s_fo, u + 1)
                    sp.dma_start(out[ds(u * U * P, U * P), :].rearrange("(u p) c -> p u c", p=P),
                                 fc[k]).then_inc(s_ost[k], 16)
            for k in range(2):
                sp.wait_ge(s_ost[k], 16 * (NU // 2))

        @block.gpsimd
        def _(pool):
            n = [0]

            def done(ins):
                n[0] += 1
                ins.then_inc(s_const, 1)

            def masked(t, pattern, op, base, cm, fill, also=None):
                pool.wait_ge(s_const, n[0])
                done(pool.affine_select(out=t, in_=t, pattern=pattern, compare_op=op, fill=fill, base=base,
                                        channel_multiplier=cm))

            pool.memset(zero, 0.0).then_inc(s_zero, 1)
            done(pool.memset(ident[:], 0.0))
            done(pool.memset(upper[:], 1.0))
            done(pool.memset(lower, 1.0))
            done(pool.memset(ones[:], 1.0))
            done(pool.memset(mask_l, 1.0))
            done(pool.memset(mask_s, 1.0))
            done(pool.memset(half0, 1.0))
            done(pool.memset(rscale, 1.0 / N))
            done(pool.memset(eps[:], EPS_LN))
            done(pool.iota(iota16[:], [[1, X]], base=0, channel_multiplier=0, allow_small_or_imprecise_dtypes=True))
            done(pool.iota(base16[:], [[R, X]], base=0, channel_multiplier=0, allow_small_or_imprecise_dtypes=True))
            done(pool.iota(dummy, [[0, 1]], base=NP, channel_multiplier=1, allow_small_or_imprecise_dtypes=True))
            masked(ident[:], [[-1, P]], ALU.not_equal, 0, 1, 1.0)
            masked(upper[:], [[1, P]], ALU.is_gt, 0, -1, 0.0)
            masked(lower, [[-1, P]], ALU.is_gt, 0, 1, 0.0)
            masked(mask_l, [[-D, 4], [0, VH]], ALU.is_ge, 0, 1, 0.0)
            masked(mask_l, [[D, 4], [0, VH]], ALU.is_ge, D - 1, -1, 0.0)
            masked(mask_s, [[-16, H], [0, VH]], ALU.is_ge, 0, 1, 0.0)
            masked(mask_s, [[16, H], [0, VH]], ALU.is_ge, 15, -1, 0.0)
            masked(half0, [[0, 1]], ALU.is_ge, -D, 1, 0.5)
            masked(rscale, [[-P, NT]], ALU.is_ge, N - 1, -1, 0.0)
            assert n[0] == NCONST

            def gather(b, j, k):
                pool.wait_ge(s_msg, EB * b + j + 1)
                pool.sem_inc(s_here, 1)
                pool.indirect_dma_start(out=gx[j], out_offset=None, in_=xn_dram,
                                        in_offset=bass.IndirectOffsetOnAxis(ap=dstb[k][:, j:j + 1], axis=0)
                                        ).then_inc(s_gath[j], 16)

            def scatter(b, j, k, first=False):
                pool.wait_ge(s_evac, 4 * b + j // 2 + 5)
                if j >= 2:
                    pool.wait_ge(s_scat[j - 2], 16 * b + 16)
                elif not first:
                    pool.wait_ge(s_scat[j + 6], 16 * b)
                pool.sem_inc(s_here, 1)
                pool.indirect_dma_start(out=acc_dram[j % 2], in_=msg[:, j, :],
                                        out_offset=bass.IndirectOffsetOnAxis(ap=idxb[k][:, j:j + 1], axis=0),
                                        in_offset=None, compute_op=ALU.add).then_inc(s_scat[j], 16)

            def turn(b, k, first=False):
                pool.wait_ge(s_prep, b + 2)
                for j in range(EB):
                    gather(b + 1, j, 1 - k)
                    if j == 0:
                        pool.wait_ge(s_idx, b + 1)
                    scatter(b, j, k, first)

            pool.wait_ge(s_xnst, 16 * NU)
            pool.wait_ge(s_prep, 1)
            for j in range(EB):
                gather(0, j, 0)
            pool.wait_ge(s_zeroed, 16 * EB)
            turn(0, 0, first=True)
            turn(1, 1)
            with pool.Fori(1, NB // 2 - 1) as i:
                turn(2 * i, 0)
                turn(2 * i + 1, 1)
            turn(NB - 2, 0)
            pool.wait_ge(s_idx, NB)
            for j in range(EB):
                scatter(NB - 1, j, 1)

            with pool.Fori(0, NU // 2) as i:
                for k in range(2):
                    pool.wait_ge(s_idxz, 2 * i + k + 1)
                    pool.sem_inc(s_here, 1)
                    for j in range(U):
                        for m in range(2):
                            pool.indirect_dma_start(out=z_dram, in_=zt5[k][:, j, :], in_offset=None,
                                                    out_offset=bass.IndirectOffsetOnAxis(ap=idxz[k][:, j, m:m + 1], axis=0)
                                                    ).then_inc(s_zsc[k], 16)
            for k in range(2):
                pool.wait_ge(s_zsc[k], 160 * (NU // 2))
            pool.memset(zeros, 0.0).then_inc(s_dz, 1)
            pool.iota(thr, [[P, NT]], base=0, channel_multiplier=0, allow_small_or_imprecise_dtypes=True).then_inc(s_dz, 1)
            pool.iota(tau, [[1, FTL]], base=0, channel_multiplier=0, allow_small_or_imprecise_dtypes=True).then_inc(s_dz, 1)
            pool.wait_ge(s_tail, 16 * (20 + X) + 1)
            with pool.Fori(0, NU // 2) as i:
                for k in range(2):
                    pool.wait_ge(s_idxc, 2 * i + k + 1)
                    pool.sem_inc(s_here, 1)
                    for j in range(U):
                        for m in range(2):
                            pool.indirect_dma_start(out=yg[k][:, m, j, :], out_offset=None, in_=y_dram,
                                                    in_offset=bass.IndirectOffsetOnAxis(ap=idxz[k][:, j, m:m + 1], axis=0)
                                                    ).then_inc(s_yg[k], 16)

        @block.scalar
        def _(act):
            act.dma_start(wqkv, wqkvT.rearrange("(c p) n -> p c n", p=P)).then_inc(s_cload, 16)
            act.dma_start(wproj, wprojT.rearrange("(c p) n -> p c n", p=P)).then_inc(s_cload, 16)
            act.dma_start(bqkv_b, bqkv.partition_broadcast(P)).then_inc(s_cload, 16)
            act.dma_start(bproj_b, bproj.partition_broadcast(P)).then_inc(s_cload, 16)
            act.dma_start(temp_b, temp.partition_broadcast(P)).then_inc(s_cload, 16)
            act.dma_start(gb_b[:], gate_b.partition_broadcast(P)).then_inc(s_cload, 16)
            act.dma_start(gw[:], gate_w.rearrange("(c p) n -> p c n", p=P)).then_inc(s_cload, 16)
            act.dma_start(b1c[:], b1T).then_inc(s_cload, 16)
            act.sem_inc(s_evac, 4)
            act.sem_inc(s_qq, 3)
            act.sem_inc(f_zTe, 2)
            act.sem_inc(f_hTe, 2)
            act.wait_ge(s_const, NCONST)
            act.wait_ge(s_cload, NCLOAD)

            def answer(q, out_, in_, func, **kw):
                act.wait_ge(s_ask, q + 1)
                act.activation(out_, in_, func, **kw).then_inc(s_act, 1)

            with act.Fori(0, NU) as u:
                answer(u, std5[:], mv[:, ds(u * U, U), 1:2].rearrange("p u o -> p (u o)"), ACT.Sqrt, bias=eps[:])

            def evac(b, q):
                act.wait_ge(s_msg, EB * b + 2 * q + 2 + EB)
                if not (isinstance(b, int) and b == 0):
                    for j in (2 * q, 2 * q + 1):
                        act.wait_ge(s_scat[j], 16 * b)
                act.activation(msg[:, 2 * q:2 * q + 2, :], ps_msg, ACT.Copy).then_inc(s_evac, 1)

            def still_xn(s, k):
                act.activation(xst[k], rows[:, ds(s, 1), :].rearrange("p o c -> p (o c)"), ACT.Copy).then_inc(s_xst, 1)

            def evac_xT(s, k):
                act.wait_ge(s_xTp, s + 1)
                act.activation(xT[k], ps_xT.rearrange("p (c n) -> p c n", c=2), ACT.Copy).then_inc(s_xT, 1)

            def key_turn(s, k, last=False):
                if not last:
                    still_xn(s + 1, 1 - k)
                act.wait_ge(s_bias, s + 2)
                act.activation(sq, qkvb[:, 0:2 * C], ACT.Square).then_inc(s_sq, 1)
                answer(NU + s, nrm, ss, ACT.Sqrt)
                act.wait_ge(s_acc, s + 1)
                act.activation(v1[k][:, :, 1:VH], qkvb[:, 2 * C:3 * C].rearrange("p (h d) -> p h d", h=H), ACT.Copy,
                               scale=rscale[:, ds(s, 1)])
                act.activation(v1[k][:, :, 0:1], ones[:, 0:H].unsqueeze(2), ACT.Copy,
                               scale=rscale[:, ds(s, 1)]).then_inc(s_v1, 1)
                evac(s, 0)
                if not last:
                    evac_xT(s + 1, 1 - k)
                for q in range(1, 4):
                    evac(s, q)

            act.wait_ge(s_xn, NU)
            still_xn(0, 0)
            evac_xT(0, 0)
            key_turn(0, 0)
            key_turn(1, 1)
            with act.Fori(1, NT // 2 - 1) as i:
                key_turn(2 * i, 0)
                key_turn(2 * i + 1, 1)
            key_turn(NT - 2, 0)
            key_turn(NT - 1, 1, last=True)

            def repeat_q(s, k):
                q = rows[:, ds(s, 1), :].rearrange("p o (h d) -> p (o h) d", h=H)
                act.activation(kd[k][:, :, 0:D], q, ACT.Copy)
                act.activation(kd[k][:, :, D:DW], q[:, :, 0:16], ACT.Copy)
                act.activation(kc[k].rearrange("p (h d) -> p h d", h=H), q, ACT.Copy).then_inc(s_qd, 1)

            def query_turn(s, k, last=False):
                for m in range(QI):
                    act.wait_ge(s_qtr, QI * s + m + 1)
                    act.wait_ge(s_yi, QI * s + m + 1)
                    w = 3 if m == 0 else KC
                    act.activation(qq[m % 3][:, 0:w, :], bank[m % 3][:, 0:w * P].rearrange("p (g n) -> p g n", g=w),
                                   ACT.Copy).then_inc(s_qq, 1)
                    if m == 1 and not last:
                        repeat_q(s + 1, 1 - k)
                    if m == 4:
                        evac(NT + s, 0)
                    if m == 7:
                        evac(NT + s, 1)
                evac(NT + s, 2)
                act.wait_ge(s_oTp, s + 1)
                act.activation(oT[k], ps_oT.rearrange("p (c n) -> p c n", c=2), ACT.Copy).then_inc(s_oT, 1)
                evac(NT + s, 3)

            act.wait_ge(s_mom, 1)
            repeat_q(0, 0)
            with act.Fori(0, NT // 2 - 1) as i:
                query_turn(2 * i, 0)
                query_turn(2 * i + 1, 1)
            query_turn(NT - 2, 0)
            query_turn(NT - 1, 1, last=True)

            def gate_root(u):
                answer(NU + NT + 2 * u, std5[:], mv[:, ds(u * U, U), 1:2].rearrange("p u o -> p (u o)"),
                       ACT.Sqrt, bias=eps[:])

            def gate_z(u, k, i):
                act.wait_ge(s_ask, NU + NT + 2 * u + 2)
                if not (isinstance(i, int) and i == 0):
                    act.wait_ge(s_zsc[k], 160 * i)
                for j in range(U):
                    t = u * U + j
                    act.activation(zt5[k][:, j, :], rows[:, ds(t, 1), :].rearrange("p o c -> p (o c)"), ACT.Identity,
                                   scale=rstd[:, ds(t, 1)], bias=nbias[:, ds(t, 1)]).then_inc(s_z, 1)
                for j in range(U):
                    g = (U * k + j) % 2
                    act.wait_ge(s_zTp, u * U + j + 1)
                    act.activation(zT[g][:], ps_zT[g].rearrange("p (c n) -> p c n", c=2), ACT.Copy).then_inc(s_zT, 1)

            for k in range(2):
                gate_root(k)
                gate_z(k, k, 0)
            with act.Fori(1, NU // 2) as i:
                for k in range(2):
                    gate_root(2 * i + k)
                    gate_z(2 * i + k, k, i)
            nq = NU + NT + 2 * NU
            act.wait_ge(s_ask, nq + 1)
            act.activation(topv[:, :, 1], topv[:, :, 1], ACT.Exp).then_inc(s_act, 1)

            def evac_zT(t, k):
                act.wait_ge(f_zT, t + 1)
                act.activation(zT[k % 2][:], ps_zT[k % 2].rearrange("p (c n) -> p c n", c=2), ACT.Copy).then_inc(f_zTe, 1)

            act.wait_ge(s_tab, 1)
            evac_zT(0, 0)
            evac_zT(1, 1)
            with act.Fori(0, FT // 4) as i:
                for k in range(4):
                    t = 4 * i + k
                    ex = act.value_load(expI[0:1, ds(t, 1)], min_val=0, max_val=X - 1)
                    act.wait_ge(f_hT, t + 1)
                    for c in range(FC):
                        a = act.activation(hT[k % 2][:, c, :], ps_hT[k % 2][:, c * P:(c + 1) * P], ACT.Relu,
                                           bias=b1c[:, ds(ex * FC + c, 1)])
                    a.then_inc(f_hTe, 1)
                    evac_zT(t + 2, k)

            with act.Fori(0, NU // 2) as i:
                for k in range(2):
                    u = 2 * i + k
                    q0 = nq + 1 + 3 * u
                    act.wait_ge(s_ask, q0 + 1)
                    for j in range(U):
                        t = u * U + j
                        a = act.activation(zc[k][:, j, :], rows[:, ds(t, 1), :].rearrange("p o c -> p (o c)"), ACT.Identity,
                                           scale=rstd[:, ds(t, 1)], bias=nbias[:, ds(t, 1)])
                    a.then_inc(s_zc, 1)
                    answer(q0 + 1, std5[:], mvc[:, :, 1], ACT.Sqrt, bias=eps[:])
                    act.wait_ge(s_ask, q0 + 3)
                    for j in range(U):
                        a = act.activation(fn[:, j, :], zc[k][:, j, :], ACT.Identity, scale=rc[:, j:j + 1],
                                           bias=nc5[:, j:j + 1])
                    a.then_inc(s_fn, 1)

        @block.vector
        def _(v):
            n = [0]
            base = [0]

            def mark(ins):
                n[0] += 1
                ins.then_inc(s_dve, 1)

            def join():
                v.wait_ge(s_dve, base[0] + n[0])

            def link(ins):
                mark(ins)
                join()

            def loop(first, last, body):
                start = base[0] + n[0]
                per = body_steps[body]
                with v.Fori(first, last) as i:
                    base[0], n[0] = start + (i - first) * per, 0
                    body(i, False)
                    assert n[0] == per, n[0]
                base[0], n[0] = start + (last - first) * per, 0

            def flat(a):
                return a.rearrange("p o c -> p (o c)")

            def tile(t):
                return flat(rows[:, ds(t, 1), :])

            v.sem_inc(s_d, 4)
            v.sem_inc(s_bias, 1)
            v.sem_inc(f_yo, 2)
            v.wait_ge(s_cload, NCLOAD)
            v.wait_ge(s_const, NCONST)
            mark(v.tensor_scalar(fac[:, 0:H], temp_b, SCALE * SCALE, None, ALU.mult))
            mark(v.memset(fac[:, H:2 * H], SCALE))
            mark(v.memset(ssc[:, 0:H], SCALE * SCALE))
            mark(v.memset(ssc[:, H:2 * H], 1.0))
            mark(v.memset(crun[:], 0.0))

            def row_stats(row, mv_of, r, q):
                for j in range(U):
                    mark(v.bn_stats(st[:, j, :], row(j)))
                join()
                v.sem_inc(s_here, 1)
                for j in range(U):
                    mark(v.bn_aggr(mv5[:, j, :], st[:, j, :]))
                join()
                link(v.tensor_copy(mv_of, mv5[:]))
                v.sem_inc(s_ask, 1)
                v.wait_ge(s_act, q + 1)
                link(v.reciprocal(r, std5[:]))

            def norm_pair(i, first):
                for k in range(2):
                    u = 2 * i + k
                    v.wait_ge(s_xin[k], 16 * (i + 1))
                    row_stats(lambda j: tile(u * U + j), mv[:, ds(u * U, U), :],
                              rstd[:, ds(u * U, U)], u)
                    for j in range(U):
                        t = u * U + j
                        a = v.tensor_scalar(tile(t), tile(t), flat(mv[:, ds(t, 1), 0:1]), rstd[:, ds(t, 1)],
                                            ALU.subtract, ALU.mult)
                    a.then_inc(s_xn, 1)

            def prep(b, k):
                if not (isinstance(b, int) and b == 0):
                    v.wait_ge(s_msg, EB * b)
                if not (isinstance(b, int) and b < 2):
                    v.wait_ge(s_idx, b - 1)
                mark(v.tensor_copy(srcb[k], flat(srcI[:, ds(b, 1), :])))
                mark(v.tensor_copy(wb[k], flat(wE[:, ds(b, 1), :])))
                v.tensor_copy(dstb[k][:], flat(dstI[:, ds(b, 1), :])).then_inc(s_prep, 1)

            def equal(b, j, k):
                if j % 4 == 0:
                    v.wait_ge(s_tr, 2 * b + j // 4 + 1)
                v.wait_ge(s_msg, EB * b + j + 1)
                v.wait_ge(s_d, EB * b + j + 1)
                v.tensor_scalar(wd[j], ps_src[:, j % 4, :], srcb[k][:, j:j + 1], wb[k][:, j:j + 1],
                                ALU.is_equal, ALU.mult)
                v.scalar_tensor_tensor(out=junk[j % 4], in0=ps_src[:, j % 4, :], scalar=srcb[k][:, j:j + 1], in1=lower,
                                       op0=ALU.is_equal, op1=ALU.mult, accum_out=cnt[:, j:j + 1]).then_inc(s_d, 1)

            def scatter_rows(b, k):
                v.wait_ge(s_d, EB * b + EB + 4)
                link(v.tensor_scalar(dup, cnt, 1.0, None, ALU.min))
                link(v.tensor_scalar(ddd, srcb[k], dummy[:, 0:1], -1.0, ALU.subtract, ALU.mult))
                link(v.tensor_tensor(ddd, ddd, dup, ALU.mult))
                v.wait_ge(s_evac, 4 * b + 4)
                v.tensor_tensor(idxb[k][:], srcb[k], ddd, ALU.add).then_inc(s_idx, 1)

            def shifted(k, h):
                return v.tensor_tensor(kk[k][:, h], window(kd[k], h * DW, [[0, 16], [1, D]]),
                                       window(kd[k], h * DW, [[1, 16], [1, D]]), ALU.mult)

            def shift16(k):
                return v.tensor_tensor(k16[k].rearrange("p (h i) -> p h i", h=H), kd[k][:, :, 0:16], kd[k][:, :, 16:32],
                                       ALU.mult)

            def key_pair(i, first):
                for k in range(2):
                    s = 2 * i + k
                    v.wait_ge(s_qkv, s + 1)
                    if not (first and k == 0):
                        v.wait_ge(s_v1, s)
                        v.wait_ge(s_kk, s)
                    v.tensor_tensor(qkvb, bqk[:, 0:3 * C], bqkv_b, ALU.add).then_inc(s_bias, 1)
                    for j in range(4):
                        equal(s, j, k)
                    v.wait_ge(s_sq, s + 1)
                    link(v.tensor_reduce(ss, sq.rearrange("p (g d) -> p g d", d=D), AX.X, ALU.add))
                    link(v.scalar_tensor_tensor(out=ss, in0=ss, scalar=1e-30, in1=ssc, op0=ALU.max, op1=ALU.mult))
                    v.sem_inc(s_ask, 1)
                    prep(s + 1, 1 - k)
                    for j in range(4, EB):
                        equal(s, j, k)
                    scatter_rows(s, k)
                    v.wait_ge(s_act, NU + s + 1)
                    link(v.tensor_scalar(nrm, nrm, EPS_N, None, ALU.max))
                    link(v.reciprocal(rn, nrm))
                    link(v.tensor_tensor(rn, rn, fac, ALU.mult))
                    qh = qkvb[:, 0:C].rearrange("p (h d) -> p h d", h=H)
                    kh = qkvb[:, C:2 * C].rearrange("p (h d) -> p h d", h=H)
                    rq = rn[:, 0:H].unsqueeze(2)
                    rk_ = rn[:, H:2 * H].unsqueeze(2)
                    v.wait_ge(s_acc, s + 1)
                    mark(v.tensor_tensor(kc[k].rearrange("p (h d) -> p h d", h=H), kh, rk_.broadcast_to([P, H, D]), ALU.mult))
                    mark(v.tensor_tensor(kd[k][:, :, 0:D], kh, rk_.broadcast_to([P, H, D]), ALU.mult))
                    link(v.tensor_tensor(kd[k][:, :, D:DW], kh[:, :, 0:16], rk_.broadcast_to([P, H, 16]), ALU.mult))
                    v.tensor_tensor(tile(s).rearrange("p (h d) -> p h d", h=H), qh, rq.broadcast_to([P, H, D]), ALU.mult)
                    for h in range(H):
                        shifted(k, h)
                    shift16(k).then_inc(s_kk, 1)
                    join()

            def query_pair(i, first):
                for k in range(2):
                    s = 2 * i + k
                    last = isinstance(s, int) and s == NT - 1

                    def next_heads(a, b):
                        if not last:
                            for h in range(a, b):
                                shifted(1 - k, h).then_inc(s_qn, 1)

                    for j in range(4):
                        equal(NT + s, j, k)
                    prep(NT + s + 1, 1 - k)
                    for j in range(4, EB):
                        equal(NT + s, j, k)
                    scatter_rows(NT + s, k)
                    if not last:
                        v.wait_ge(s_qd, s + 2)
                        shift16(1 - k).then_inc(s_qn, 1)
                    next_heads(0, 3)
                    v.wait_ge(s_yi, QI * s + QI + 3)
                    link(v.tensor_tensor(yb.rearrange("p h e -> p (h e)"), ps_y, m0, ALU.add))
                    link(v.reciprocal(yr, yb[:, :, 0]))
                    v.tensor_tensor(on[k].rearrange("p (h d) -> p h d", h=H), yb[:, :, 1:VH],
                                    yr.unsqueeze(2).broadcast_to([P, H, D]), ALU.mult).then_inc(s_on, 1)
                    next_heads(3, 7)
                    v.wait_ge(s_pr, s + 1)
                    v.wait_ge(s_xr[k], 16 * (i + 1))
                    link(v.tensor_tensor(pr, ps_pr, bproj_b, ALU.add))
                    v.tensor_tensor(tile(s), pr, xin[k], ALU.add).then_inc(s_x1, 1)
                    next_heads(7, 8)

            def gate_front(u):
                mine = rows[:, ds(u * U, U), :]
                v.wait_ge(s_accl, 32 * (u + 1))
                link(v.tensor_tensor(mine, mine, accb[:, 0], ALU.add))
                link(v.tensor_tensor(mine, mine, accb[:, 1], ALU.add))
                v.sem_inc(s_bx, 1)
                row_stats(lambda j: tile(u * U + j), mv[:, ds(u * U, U), :], rstd[:, ds(u * U, U)], NU + NT + u)
                link(v.scalar_tensor_tensor(out=nbias[:, ds(u * U, U)],
                                            in0=mv[:, ds(u * U, U), 0:1].rearrange("p u o -> p (u o)"), scalar=-1.0,
                                            in1=rstd[:, ds(u * U, U)], op0=ALU.mult, op1=ALU.mult))
                v.sem_inc(s_ask, 1)

            def gate_back(u, k):
                v.wait_ge(s_lg, u + 1)
                link(v.tensor_tensor(lg[:], ps_lg[k].rearrange("p (u e) -> p u e", u=U),
                                     gb_b[:].unsqueeze(1).broadcast_to([P, U, X]), ALU.add))
                v.sem_inc(s_here, 1)
                for j in range(U):
                    mark(v.max(m8[:, j, :], lg[:, j, :]))
                join()
                v.sem_inc(s_here, 1)
                for j in range(U):
                    mark(v.max_index(i8[:, j, :], m8[:, j, :], lg[:, j, :]))
                mark(v.tensor_copy(topv[:, ds(u * U, U), :], m8[:, :, 0:2]))
                join()
                link(v.tensor_copy(idf[:], i8[:, :, 0:2]))
                for m in range(2):
                    mark(v.tensor_tensor(oh[m], iota16[:].unsqueeze(1).broadcast_to([P, U, X]),
                                         idf[:, :, m:m + 1].broadcast_to([P, U, X]), ALU.is_equal))
                join()
                link(v.tensor_tensor(cc, oh[0], oh[1], ALU.add))
                v.sem_inc(s_cc, 1)
                mark(v.tensor_reduce(csum[:], cc.rearrange("p u e -> p e u"), AX.X, ALU.add))
                v.wait_ge(s_rk, u + 1)
                join()
                mark(v.tensor_tensor(crun[:], crun[:], csum[:], ALU.add))
                link(v.tensor_tensor(rk, ps_rk.rearrange("p (u e) -> p u e", u=U),
                                     base16[:].unsqueeze(1).broadcast_to([P, U, X]), ALU.add))
                for m in range(2):
                    link(v.tensor_tensor(pk, rk, oh[m], ALU.mult))
                    link(v.tensor_reduce(posf[:, :, m:m + 1], pk, AX.X, ALU.add))
                mark(v.tensor_copy(posT[:, ds(u * U, U), :], posf[:]))
                mark(v.tensor_copy(expT[:, ds(u * U, U), :], idf[:]))
                v.tensor_copy(idxz[k][:], posf[:]).then_inc(s_idxz, 1)

            def gate_pair(i, first):
                for k in range(2):
                    u = 2 * i + k
                    if not (isinstance(u, int) and u == NU - 1):
                        gate_front(u + 1)
                    if not first:
                        v.wait_ge(s_zsc[k], 160 * i)
                    gate_back(u, k)

            def combine_pair(i, first):
                for k in range(2):
                    u = 2 * i + k
                    v.sem_inc(s_ask, 1)
                    v.wait_ge(s_yg[k], 160 * (i + 1))
                    v.wait_ge(s_zc, u + 1)
                    for m in range(2):
                        for j in range(U):
                            mark(v.scalar_tensor_tensor(out=zc[k][:, j, :], in0=yg[k][:, m, j, :],
                                                        scalar=flat(topv[:, ds(u * U + j, 1), m:m + 1]),
                                                        in1=zc[k][:, j, :], op0=ALU.mult, op1=ALU.add))
                        join()
                    if not (isinstance(i, int) and i == NU // 2 - 1):
                        v.tensor_copy(idxz[k][:], posT[:, ds((u + 2) * U, U), :]).then_inc(s_idxc, 1)
                    row_stats(lambda j: zc[k][:, j, :], mvc, rc, NU + NT + NU + 1 + u)
                    link(v.scalar_tensor_tensor(out=nc5, in0=mvc[:, :, 0], scalar=-1.0, in1=rc,
                                                op0=ALU.mult, op1=ALU.mult))
                    v.sem_inc(s_ask, 1)
                    v.wait_ge(s_fn, u + 1)
                    link(v.tensor_tensor(fn, fn, gamma_b.unsqueeze(1).broadcast_to([P, U, C]), ALU.mult))
                    if not first:
                        v.wait_ge(s_ost[k], 16 * i)
                    link(v.tensor_tensor(fc[k], fn, beta_b.unsqueeze(1).broadcast_to([P, U, C]), ALU.add))
                    v.tensor_tensor(fc[k], fc[k], rows[:, ds(u * U, U), :], ALU.add).then_inc(s_fo, 1)

            body_steps = {
                norm_pair: 2 * (2 * U + 2),
                key_pair: 2 * (2 + 3 + 3 + 3 + 2),
                query_pair: 2 * (2 + 3 + 2 + 1),
                gate_pair: 2 * (2 + 2 * U + 2 + 1 + 1 + U + U + 1 + 1 + 2 + 1 + 1 + 2 + 4 + 2),
                combine_pair: 2 * (2 * U + 2 * U + 2 + 1 + 2),
            }

            loop(0, NU // 2, norm_pair)
            v.wait_ge(s_etab, 48)
            v.wait_ge(s_xnst, 16 * NU)
            v.wait_ge(s_zeroed, 16 * EB)
            prep(0, 0)
            join()
            key_pair(0, True)
            loop(1, NT // 2, key_pair)

            v.wait_ge(s_acc, NT + 2)
            mark(v.tensor_copy(m2[:, 0:15, :], bank[0][:, 0:15 * VH].rearrange("p (c e) -> p c e", e=VH)))
            mark(v.tensor_copy(m2[:, 15:30, :], bank[1][:, 0:15 * VH].rearrange("p (c e) -> p c e", e=VH)))
            mark(v.tensor_copy(m2[:, 30:32, :], bank[2][:, 0:2 * VH].rearrange("p (c e) -> p c e", e=VH)))
            for g in range(2):
                mark(v.scalar_tensor_tensor(out=m1[:, g, :], in0=sum_k[g], scalar=SCALE ** 2,
                                            in1=mask_l.rearrange("p a b -> p (a b)"), op0=ALU.mult, op1=ALU.mult))
                mark(v.tensor_tensor(m16[:, W4 * g:W4 * (g + 1)], sum_16[g],
                                     mask_s.rearrange("p a b -> p (a b)")[:, W4 * g:W4 * (g + 1)], ALU.mult))
                mark(v.tensor_scalar(m0[:, W4 * g:W4 * (g + 1)], sum_v[g], SCALE ** 4, None, ALU.mult))
            join()
            shift0 = m2.rearrange("p (h g) e -> p h g e", g=KC)[:, :, 0, :]
            link(v.tensor_scalar(shift0, shift0, half0[:, 0:1], None, ALU.mult))
            v.sem_inc(s_mom, 1)
            v.wait_ge(s_qd, 1)
            shift16(0).then_inc(s_qn, 1)
            for h in range(H):
                shifted(0, h).then_inc(s_qn, 1)
            loop(0, NT // 2 - 1, query_pair)
            query_pair(NT // 2 - 1, False)
            gate_front(0)
            gate_pair(0, True)
            loop(1, NU // 2 - 1, gate_pair)
            gate_pair(NU // 2 - 1, False)

            join()
            link(v.tensor_tensor(topv[:, :, 1], topv[:, :, 1], topv[:, :, 0], ALU.subtract))
            v.sem_inc(s_cc, 1)
            v.sem_inc(s_ask, 1)
            v.wait_ge(s_act, NU + NT + NU + 1)
            link(v.tensor_scalar(topv[:, :, 0], topv[:, :, 1], 1.0, None, ALU.add))
            link(v.reciprocal(topv[:, :, 0], topv[:, :, 0]))
            link(v.tensor_tensor(topv[:, :, 1], topv[:, :, 1], topv[:, :, 0], ALU.mult))

            v.wait_ge(s_cnt, 1)
            for k in range(2):
                v.wait_ge(s_zsc[k], 160 * (NU // 2))
            v.wait_ge(s_dz, 3)
            link(v.tensor_copy(cntR[:], ps_cnt))
            link(v.tensor_tensor(cmpc, cntR[:].unsqueeze(2).broadcast_to([P, X, NT]),
                                 thr.unsqueeze(1).broadcast_to([P, X, NT]), ALU.is_gt))
            link(v.tensor_reduce(ntl, cmpc, AX.X, ALU.add))
            link(v.tensor_tensor_scan(endt, ones[:, 0:X], ntl, 0.0, ALU.mult, ALU.add))
            link(v.tensor_tensor(shift, endt, ntl, ALU.subtract))
            link(v.scalar_tensor_tensor(out=shift, in0=shift, scalar=float(P), in1=base16[:], op0=ALU.mult, op1=ALU.subtract))
            link(v.tensor_tensor(cmpy, expT[:].rearrange("p t k -> p (t k)").unsqueeze(2).broadcast_to([P, 2 * NT, X]),
                                 iota16[:].unsqueeze(1).broadcast_to([P, 2 * NT, X]), ALU.is_equal))
            link(v.tensor_tensor(cmpy, cmpy, shift.unsqueeze(1).broadcast_to([P, 2 * NT, X]), ALU.mult))
            link(v.tensor_reduce(expT[:].rearrange("p t k -> p (t k)"), cmpy, AX.X, ALU.add))
            link(v.tensor_tensor(posT[:], posT[:], expT[:], ALU.add))
            link(v.tensor_tensor(cmpt, endt[0:1, :].unsqueeze(1).broadcast_to([1, FTL, X]),
                                 tau.unsqueeze(2).broadcast_to([1, FTL, X]), ALU.is_le))
            link(v.tensor_reduce(etau, cmpt, AX.X, ALU.add))
            link(v.tensor_tensor(cmpm, cmpt, ntl[0:1, :].unsqueeze(1).broadcast_to([1, FTL, X]), ALU.mult))
            link(v.tensor_reduce(stau, cmpm, AX.X, ALU.add))
            link(v.tensor_tensor(stau, tau, stau, ALU.subtract))
            link(v.tensor_scalar(rowf, etau, float(R), None, ALU.mult))
            link(v.scalar_tensor_tensor(out=rowf, in0=stau, scalar=float(P), in1=rowf, op0=ALU.mult, op1=ALU.add))
            mark(v.tensor_copy(rowI, rowf))
            mark(v.tensor_scalar(expI, etau, float(X - 1), None, ALU.min))
            link(v.tensor_tensor(tailI[:], cntR[0:1, :], base16[0:1, :], ALU.add))
            v.sem_inc(s_tab, 1)

            def copy_h(t, k):
                v.wait_ge(f_h, t + 1)
                v.tensor_copy(hs[k % 2], ps_h[k % 2][:]).then_inc(f_hs, 1)

            def expert_four(i, first):
                for k in range(4):
                    t = 4 * i + k
                    copy_h(t + 1, k + 1)
                    v.wait_ge(f_y, t + 1)
                    v.wait_ge(s_b2in[k], 16 * (i + 1))
                    if not first:
                        v.wait_ge(s_yst[k], 16 * i)
                    v.tensor_tensor(yo[k], ps_y2[k % 2], b2t[k], ALU.add).then_inc(f_yo, 1)

            body_steps[expert_four] = 0
            copy_h(0, 0)
            expert_four(0, True)
            loop(1, FT // 4, expert_four)

            v.wait_ge(s_gb, 32)
            for k in range(2):
                v.tensor_copy(idxz[k][:], posT[:, k * U:(k + 1) * U, :]).then_inc(s_idxc, 1)
            combine_pair(0, True)
            loop(1, NU // 2 - 1, combine_pair)
            combine_pair(NU // 2 - 1, False)

        @block.tensor
        def _(pe):
            pe.sem_inc(s_msg, EB)
            pe.sem_inc(s_acc, 2)
            pe.sem_inc(s_yi, 3)
            pe.wait_ge(s_const, NCONST)
            pe.wait_ge(s_cload, NCLOAD)

            def turn_src(b, g, k):
                pe.wait_ge(s_d, EB * b + 4 * g + 4)
                for j in range(4):
                    a = pe.transpose(ps_src[:, j, :], srcb[k][:, 4 * g + j:4 * g + j + 1].broadcast_to([P, P]), ident[:])
                a.then_inc(s_tr, 1)

            def message(b, q):
                pe.wait_ge(s_evac, 4 * b + q + 4)
                for j in (2 * q, 2 * q + 1):
                    pe.wait_ge(s_d, EB * b + j + 5)
                    pe.wait_ge(s_gath[j], 16 * (b + 1))
                    pe.matmul(ps_msg[:, j % 2, :], wd[j], gx[j], start=True, stop=True).then_inc(s_msg, 1)

            def moments(s, k, part_, first=False):
                started = set() if first else {0, 1, 2, 3}

                def add(b, out_, lhsT, rhs):
                    a = pe.matmul(out_, lhsT, rhs, start=b not in started, stop=False, skip_group_check=True)
                    started.add(b)
                    return a

                if part_ == 0:
                    pe.wait_ge(s_kk, s + 1)
                    pe.wait_ge(s_v1, s + 1)
                for h in ((0, 1), (2, 3, 4), (5, 6, 7))[part_]:
                    for g in range(KC):
                        c = h * KC + g
                        if first and c in (4 * 2, 4 * 5) and c // 15 == (c - 1) // 15:
                            started.add(c // 15)
                        add(c // 15, chunk_out(c), kk[k][:, h, 4 * g:4 * g + 4, :].rearrange("p s i -> p (s i)"), v1[k][:, h, :])
                if part_ == 2:
                    va = v1[k].rearrange("p h e -> p (h e)")
                    for g in range(2):
                        cols = va[:, W4 * g:W4 * (g + 1)]
                        add(2, sum_k[g], kc[k][:, g * P:(g + 1) * P], cols)
                        add(3, sum_16[g], k16[k], cols)
                        a = add(2 if g == 0 else 3, sum_v[g], ones[:], cols)
                    a.then_inc(s_acc, 1)

            def turn_xn(s, k):
                pe.wait_ge(s_xst, s + 1)
                pe.wait_ge(s_bias, s + 1)
                for c in range(2):
                    a = pe.transpose(ps_xT[:, c * P:(c + 1) * P], xst[k][:, c * P:(c + 1) * P], ident[:])
                a.then_inc(s_xTp, 1)

            def project_in(s, k):
                pe.wait_ge(s_xT, s + 1)
                for lo, hi in ((0, 512), (512, 3 * C)):
                    for c in range(2):
                        a = pe.matmul(bqk[:, lo:hi], xT[k][:, c, :], wqkv[:, c, lo:hi], start=(c == 0), stop=(c == 1))
                a.then_inc(s_qkv, 1)

            def key_turn(s, k, first=False, second=False, last=False):
                pe.wait_ge(s_prep, s + 1)
                turn_src(s, 0, k)
                if not first:
                    moments(s - 1, 1 - k, 0, second)
                message(s, 0)
                turn_src(s, 1, k)
                if not last:
                    turn_xn(s + 1, 1 - k)
                message(s, 1)
                if not first:
                    moments(s - 1, 1 - k, 1, second)
                if not last:
                    project_in(s + 1, 1 - k)
                message(s, 2)
                if not first:
                    moments(s - 1, 1 - k, 2, second)
                message(s, 3)

            turn_xn(0, 0)
            project_in(0, 0)
            key_turn(0, 0, first=True)
            key_turn(1, 1, second=True)
            with pe.Fori(1, NT // 2 - 1) as i:
                for k in range(2):
                    key_turn(2 * i + k, k)
            key_turn(NT - 2, 0)
            key_turn(NT - 1, 1, last=True)
            for part_ in range(3):
                moments(NT - 1, 1, part_)

            pe.wait_ge(s_mom, 1)

            def query_item(s, m, k):
                pe.wait_ge(s_qq, QI * s + m + 1)
                pe.wait_ge(s_qn, QI * s + m + 1)
                if m == 0:
                    parts = [k16[k], kc[k][:, 0:P], kc[k][:, P:2 * P]]
                else:
                    parts = [kk[k][:, m - 1, 4 * g:4 * g + 4, :].rearrange("p s i -> p (s i)") for g in range(KC)]
                for g, src in enumerate(parts):
                    a = pe.transpose(bank[m % 3][:, g * P:(g + 1) * P], src, ident[:])
                a.then_inc(s_qtr, 1)

            def sum_item(s, m, k):
                pe.wait_ge(s_qq, QI * s + m + 4)
                if m == 0:
                    pe.matmul(ps_y, qq[0][:, 0, :], m16, start=True, stop=False, skip_group_check=True)
                    for g in range(2):
                        a = pe.matmul(ps_y[:, W4 * g:W4 * (g + 1)], qq[0][:, 1 + g, :], m1[:, g, :], start=False, stop=False,
                                      skip_group_check=True)
                else:
                    h = m - 1
                    for g in range(KC):
                        a = pe.matmul(ps_y[:, VH * h:VH * (h + 1)], qq[m % 3][:, g, :], m2[:, KC * h + g, :], start=False,
                                      stop=(m == QI - 1 and g == KC - 1), skip_group_check=True)
                a.then_inc(s_yi, 1)

            with pe.Fori(0, NT // 2) as i:
                for k in range(2):
                    s = 2 * i + k
                    pe.wait_ge(s_prep, NT + s + 1)
                    turn_src(NT + s, 0, k)
                    for m in range(QI):
                        query_item(s, m, k)
                        if m >= 2:
                            sum_item(s, m - 2, k)
                        if m == 3:
                            message(NT + s, 0)
                            turn_src(NT + s, 1, k)
                        if m == 6:
                            message(NT + s, 1)
                    sum_item(s, QI - 2, k)
                    sum_item(s, QI - 1, k)
                    message(NT + s, 2)
                    pe.wait_ge(s_on, s + 1)
                    for c in range(2):
                        a = pe.transpose(ps_oT[:, c * P:(c + 1) * P], on[k][:, c * P:(c + 1) * P], ident[:])
                    a.then_inc(s_oTp, 1)
                    message(NT + s, 3)
                    pe.wait_ge(s_oT, s + 1)
                    for c in range(2):
                        a = pe.matmul(ps_pr, oT[k][:, c, :], wproj[:, c, :], start=(c == 0), stop=(c == 1))
                    a.then_inc(s_pr, 1)

            def logits(u, k):
                def turn(j):
                    g = (U * k + j) % 2
                    pe.wait_ge(s_z, u * U + j + 1)
                    for c in range(2):
                        a = pe.transpose(ps_zT[g][:, c * P:(c + 1) * P], zt5[k][:, j, c * P:(c + 1) * P], ident[:])
                    a.then_inc(s_zTp, 1)

                turn(0)
                for j in range(U):
                    if j < U - 1:
                        turn(j + 1)
                    pe.wait_ge(s_zT, u * U + j + 1)
                    for c in range(2):
                        a = pe.matmul(ps_lg[k][:, j * X:(j + 1) * X], zT[(U * k + j) % 2][:, c, :], gw[:, c, :],
                                      start=(c == 0), stop=(c == 1))
                a.then_inc(s_lg, 1)

            def rank(u):
                pe.wait_ge(s_cc, u + 1)
                pe.matmul(ps_rk, upper[:], cc.rearrange("p u e -> p (u e)"), start=True, stop=False, skip_group_check=True)
                pe.matmul(ps_rk.rearrange("p (u e) -> p u e", u=U), ones[:], crun[:].unsqueeze(1).broadcast_to([P, U, X]),
                          start=False, stop=False, skip_group_check=True)
                for j in range(U - 1):
                    later = U - 1 - j
                    a = pe.matmul(ps_rk[:, (j + 1) * X:U * X].rearrange("p (u e) -> p u e", u=later), ones[:],
                                  cc[:, j:j + 1, :].broadcast_to([P, later, X]), start=False, stop=(j == U - 2),
                                  skip_group_check=True)
                a.then_inc(s_rk, 1)

            logits(0, 0)
            with pe.Fori(0, NU // 2 - 1) as i:
                for k in range(2):
                    rank(2 * i + k)
                    logits(2 * i + k + 1, 1 - k)
            rank(NU - 2)
            logits(NU - 1, 1)
            rank(NU - 1)
            pe.wait_ge(s_cc, NU + 1)
            pe.matmul(ps_cnt, ones[:], crun[:], start=True, stop=True).then_inc(s_cnt, 1)

            def turn_z(t, k):
                pe.transpose(ps_zT[k % 2][:, 0:P], zt[k % 4][:, 0:P], ident[:])
                pe.transpose(ps_zT[k % 2][:, P:2 * P], zt[k % 4][:, P:2 * P], ident[:]).then_inc(f_zT, 1)

            def hidden(t, k):
                ex = pe.value_load(expI[0:1, ds(t, 1)], min_val=0, max_val=X - 1)
                pe.wait_ge(f_zTe, t + 3)
                for c in range(2):
                    a = pe.matmul(ps_h[k % 2][:], zT[k % 2][:, c, :], w1s[:, ds(ex, 1), c, :].rearrange("p o f -> p (o f)"),
                                  start=(c == 0), stop=(c == 1))
                a.then_inc(f_h, 1)

            pe.wait_ge(s_tab, 1)
            pe.wait_ge(s_w, 16 * 8)
            for k in range(2):
                pe.wait_ge(s_ztin[k], 16)
                turn_z(k, k)
            hidden(0, 0)
            with pe.Fori(0, FT // 4) as i:
                for k in range(4):
                    t = 4 * i + k
                    pe.wait_ge(f_hs, t + 1)
                    pe.wait_ge(f_hTe, t + 1)
                    for c in range(FC):
                        a = pe.transpose(ps_hT[k % 2][:, c * P:(c + 1) * P], hs[k % 2][:, c * P:(c + 1) * P], ident[:])
                    a.then_inc(f_hT, 1)
                    hidden(t + 1, k + 1)
                    pe.wait_ge(s_ztin[(k + 2) % 4], 16 * (i + 1 + (k + 2) // 4))
                    turn_z(t + 2, k + 2)
                    ex = pe.value_load(expI[0:1, ds(t, 1)], min_val=0, max_val=X - 1)
                    pe.wait_ge(f_hTe, t + 3)
                    pe.wait_ge(f_yo, t + 1)
                    for c in range(FC):
                        a = pe.matmul(ps_y2[k % 2], hT[k % 2][:, c, :], w2s[:, ds(ex, 1), c, :].rearrange("p o f -> p (o f)"),
                                      start=(c == 0), stop=(c == FC - 1))
                    a.then_inc(f_y, 1)


def kernel(x, src, dst, edge_weight, L0_mix_Wqkv, L0_mix_bqkv, L0_mix_Wproj, L0_mix_bproj, L0_mix_temperature,
           L0_ffn_gate_w, L0_ffn_gate_b, L0_ffn_w1, L0_ffn_b1, L0_ffn_w2, L0_ffn_b2, L0_ffn_gamma, L0_ffn_beta):
    import numpy as np
    import concourse.bacc as bacc
    from concourse.bass_utils import run_bass_kernel_spmd

    def edges(a):
        a = np.asarray(a)
        full = np.zeros(((NB + 1) * EB * P,), a.dtype)
        full[:E] = a
        return np.ascontiguousarray(full.reshape(-1, P).T)

    xp = np.zeros((NP, C), np.float32)
    xp[:N] = np.asarray(x)
    arrays = {
        "x_pad": xp, "src_t": edges(src), "dst_t": edges(dst), "w_t": edges(edge_weight),
        "wqkv_t": np.ascontiguousarray(np.asarray(L0_mix_Wqkv).T), "bqkv": np.asarray(L0_mix_bqkv),
        "wproj_t": np.ascontiguousarray(np.asarray(L0_mix_Wproj).T), "bproj": np.asarray(L0_mix_bproj),
        "temperature": np.asarray(L0_mix_temperature).reshape(H),
        "gate_w": np.asarray(L0_ffn_gate_w), "gate_b": np.asarray(L0_ffn_gate_b), "w1": np.asarray(L0_ffn_w1),
        "b1_t": np.ascontiguousarray(np.asarray(L0_ffn_b1).reshape(X, FC, P).transpose(2, 0, 1).reshape(P, X * FC)),
        "w2": np.asarray(L0_ffn_w2), "b2": np.asarray(L0_ffn_b2), "gamma": np.asarray(L0_ffn_gamma),
        "beta": np.asarray(L0_ffn_beta),
    }
    nc = bacc.Bacc("TRN2", target_bir_lowering=False, num_devices=1)
    args = [nc.dram_tensor(k, a.shape, mybir.dt.from_np(a.dtype), kind="ExternalInput").ap() for k, a in arrays.items()]
    args.append(nc.dram_tensor("y_out", (NP, C), F32, kind="ExternalOutput").ap())
    program(nc, *args)
    r = run_bass_kernel_spmd(nc, [arrays], core_ids=[0])
    return r.results[0]["y_out"][:N]
```

```python
from contextlib import ExitStack

import concourse.bass as bass
from concourse import mybir

ALU = mybir.AluOpType
ACT = mybir.ActivationFunctionType
AX = mybir.AxisListType
F32 = mybir.dt.float32
I32 = mybir.dt.int32
U32 = mybir.dt.uint32

P = 128
N = 6250
E = 100000
C = 256
H, D = 8, 32
X = 16
F = 512
FC = F // P
NT = 50
NP = NT * P
EB = 8
NB = 2 * NT
assert NT * P >= N and NB * EB * P >= E
DW = 48
VH = D + 1
KC = 4
NACC = 2
AR = NP + P
SCALE = float(D) ** 0.25
EPS_N = 1e-12
EPS_LN = 1e-5
U = 5
NU = NT // U
R = NP + P
FT = 116
FTL = FT + 4
assert FT >= (2 * NP + X * (P - 1)) // P
ZR = X * R + 20 * P


def program(nc, x, srcT, dstT, wT, wqkvT, bqkv, wprojT, bproj, temp, gate_w, gate_b, w1, b1T, w2, b2,
            gamma, beta, out):
    with ExitStack() as ctx:
        def sb(name, shape, dt=F32):
            return ctx.enter_context(nc.sbuf_tensor(name, shape, dt))

        def sem(name):
            return ctx.enter_context(nc.semaphore(name))

        def sems(name, n):
            return [sem(f"{name}{i}") for i in range(n)]

        ds = bass.ds

        def window(t, offset, dims):
            a = t
            return bass.AP(tensor=a.tensor, offset=a.offset + offset, ap=[list(a.ap[0])] + dims)

        xn_dram = nc.dram_tensor("xn_dram", [NP, C], F32).ap()
        acc_dram = [nc.dram_tensor(f"acc_dram{k}", [AR, C], F32).ap() for k in range(NACC)]
        z_dram = nc.dram_tensor("z_dram", [ZR, C], F32).ap()
        y_dram = nc.dram_tensor("y_dram", [FT * P, C], F32).ap()

        rows = sb("rows", [P, NT, C])
        ident = sb("ident", [P, P])
        upper = sb("upper", [P, P])
        ones = sb("ones", [P, P])
        eps = sb("eps", [P, 1])
        gw = sb("gw", [P, 2, X])
        gb_b = sb("gb_b", [P, X])
        b1c = sb("b1c", [P, X * FC])
        iota16 = sb("iota16", [P, X])
        base16 = sb("base16", [P, X])
        mv = sb("mv", [P, NT, 2])
        rstd = sb("rstd", [P, NT])
        nbias = sb("nbias", [P, NT])
        topv = sb("topv", [P, NT, 2])
        posT = sb("posT", [P, NT, 2])
        expT = sb("expT", [P, NT, 2])
        crun = sb("crun", [P, X])
        st = sb("st", [P, U, 6])
        mv5 = sb("mv5", [P, U, 2])
        std5 = sb("std5", [P, U])

        big = sb("big", [P, 2 * X * 1024])
        used = [0]

        def part(shape, dt=F32):
            n = 1
            for k in shape[1:]:
                n *= k
            a = big[:, used[0]:used[0] + n]
            used[0] += n
            if dt != F32:
                a = a.bitcast(dt)
            if len(shape) == 3:
                a = a.rearrange("p (a b) -> p a b", a=shape[1])
            if len(shape) == 4:
                a = a.rearrange("p (a b c) -> p a b c", a=shape[1], b=shape[2])
            return a

        srcI = part([P, NB + 1, EB], I32)
        dstI = part([P, NB + 1, EB], I32)
        wE = part([P, NB + 1, EB])
        wqkv = part([P, 2, 3 * C])
        wproj = part([P, 2, C])
        bqkv_b = part([P, 3 * C])
        bproj_b = part([P, C])
        lower = part([P, P])
        mask_l = part([P, 4, VH])
        mask_s = part([P, H, VH])
        half0 = part([P, 1])
        rscale = part([P, NT])
        temp_b = part([P, H])
        fac = part([P, 2 * H])
        ssc = part([P, 2 * H])
        dummy = part([P, 1])
        xst = [part([P, C]) for _ in range(2)]
        xT = [part([P, 2, P]) for _ in range(2)]
        qkvb = part([P, 3 * C])
        sq = part([P, 2 * C])
        ss = part([P, 2 * H])
        nrm = part([P, 2 * H])
        rn = part([P, 2 * H])
        kd = [part([P, H, DW]) for _ in range(2)]
        kc = [part([P, C]) for _ in range(2)]
        v1 = [part([P, H, VH]) for _ in range(2)]
        kk = [part([P, H, 16, D]) for _ in range(2)]
        k16 = [part([P, P]) for _ in range(2)]
        m2 = part([P, H * KC, VH])
        m1 = part([P, 2, 4 * VH])
        m16 = part([P, H * VH])
        m0 = part([P, H * VH])
        srcb = [part([P, EB]) for _ in range(2)]
        wb = [part([P, EB]) for _ in range(2)]
        dstb = [sb(f"dstb{k}", [P, EB], I32) for k in range(2)]
        idxb = [sb(f"idxb{k}", [P, EB], I32) for k in range(2)]
        cnt = part([P, EB])
        dup = part([P, EB])
        ddd = part([P, EB])
        wd = [part([P, P]) for _ in range(EB)]
        junk = [part([P, P]) for _ in range(4)]
        qq = [part([P, 4, P]) for _ in range(3)]
        yb = part([P, H, VH])
        yr = part([P, H])
        on = [part([P, C]) for _ in range(2)]
        oT = [part([P, 2, P]) for _ in range(2)]
        xin = [part([P, C]) for _ in range(2)]
        pr = part([P, C])
        assert used[0] <= 2 * X * 1024
        gx = [part([P, C]) for k in range(EB)]
        msg = part([P, EB, C])
        assert used[0] <= 2 * X * 1024
        w1s = big[:, 0:X * 1024].rearrange("p (e c f) -> p e c f", e=X, c=2)
        w2s = big[:, X * 1024:2 * X * 1024].rearrange("p (e c f) -> p e c f", e=X, c=FC)

        mid = sb("mid", [P, 5120])
        zero = mid[:, 0:U * C]
        accb = mid[:, 0:2 * U * C].rearrange("p (k u c) -> p k u c", k=2, u=U)
        zt5 = [mid[:, 2560 + 1280 * k:3840 + 1280 * k].rearrange("p (u c) -> p u c", u=U) for k in range(2)]
        zT = [sb(f"zT{k}", [P, 2, P]) for k in range(2)]
        lg = sb("lg", [P, U, X])
        m8 = sb("m8", [P, U, 8])
        i8 = sb("i8", [P, U, 8], U32)
        idf = sb("idf", [P, U, 2])
        ranks = sb("ranks", [P, 5, U * X])
        oh = [ranks[:, k, :].rearrange("p (u e) -> p u e", u=U) for k in range(2)]
        cc, rk, pk = (ranks[:, k, :].rearrange("p (u e) -> p u e", u=U) for k in (2, 3, 4))
        csum = sb("csum", [P, X])
        posf = sb("posf", [P, U, 2])
        idxz = [sb(f"idxz{k}", [P, U, 2], I32) for k in range(2)]
        zeros = mid[:, 2304:2304 + C]
        zt = [mid[:, 256 * k:256 * (k + 1)] for k in range(4)]
        b2t = [mid[:, 1024 + 256 * k:1280 + 256 * k] for k in range(2)]
        yo = [mid[:, 1536 + 256 * k:1792 + 256 * k] for k in range(2)]
        w1c = [mid[:, 2048 + 1024 * k:3072 + 1024 * k].rearrange("p (c f) -> p c f", c=2) for k in range(2)]
        hT = [mid[:, 4096 + 512 * k:4608 + 512 * k].rearrange("p (c n) -> p c n", c=FC) for k in range(2)]
        cntR = sb("cntR", [P, X])
        ntl = lg[:, 0, :]
        endt = lg[:, 1, :]
        shift = lg[:, 2, :]
        cmpy = mid[:, 3072:3072 + NT * 2 * X].rearrange("p (t e) -> p t e", e=X)
        cmpt = mid[0:1, 0:FTL * X].rearrange("p (t e) -> p t e", e=X)
        cmpc = mid[:, 0:X * NT].rearrange("p (e j) -> p e j", e=X)
        tau = mid[0:1, 1920:1920 + FTL]
        thr = mid[:, 2040:2040 + NT]
        etau = mid[0:1, 2096:2096 + FTL]
        rowI = ranks[0:1, :, :].rearrange("p a b -> p (a b)")[:, 0:FTL].bitcast(I32)
        expI = ranks[0:1, :, :].rearrange("p a b -> p (a b)")[:, FTL:2 * FTL].bitcast(I32)
        stau = ranks[0:1, :, :].rearrange("p a b -> p (a b)")[:, 2 * FTL:3 * FTL]
        tailI = sb("tailI", [1, X], I32)

        yg = [big[:, 2560 * k:2560 * (k + 1)].rearrange("p (k u c) -> p k u c", k=2, u=U) for k in range(2)]
        zc = [big[:, 5120 + 1280 * k:6400 + 1280 * k].rearrange("p (u c) -> p u c", u=U) for k in range(2)]
        fc = [big[:, 7680 + 1280 * k:8960 + 1280 * k].rearrange("p (u c) -> p u c", u=U) for k in range(2)]
        fn = [big[:, a:a + U * C].rearrange("p (u c) -> p u c", u=U) for a in (10240, 12064)]
        gamma_b = big[:, 11520:11776]
        beta_b = big[:, 11776:12032]
        rc = big[:, 12048:12048 + U]
        nc5 = big[:, 12056:12056 + U]

        bank = [ctx.enter_context(nc.psum_tensor(f"bank{k}", [P, 512], F32)) for k in range(4)]
        bqk = ctx.enter_context(nc.psum_tensor("bqk", [P, 1024], F32))
        b6 = ctx.enter_context(nc.psum_tensor("b6", [P, 512], F32))
        b7 = ctx.enter_context(nc.psum_tensor("b7", [P, 512], F32))
        ps_src = b6[:].rearrange("p (j e) -> p j e", j=4)
        ps_xT = bqk[:, 0:C]
        ps_msg = b7[:].rearrange("p (j c) -> p j c", j=2)

        def chunk_out(c):
            return bank[c // 15][:, (c % 15) * VH:(c % 15 + 1) * VH]

        W4 = 4 * VH
        sum_k = [bank[2][:, 66 + W4 * g:66 + W4 * (g + 1)] for g in range(2)]
        sum_v = [bank[2][:, 66 + 2 * W4:66 + 3 * W4], bank[3][:, 2 * W4:3 * W4]]
        sum_16 = [bank[3][:, W4 * g:W4 * (g + 1)] for g in range(2)]
        ps_y = bqk[:, 0:H * VH]
        ps_pr = bank[3][:, 0:C]
        ps_oT = bank[3][:, C:2 * C]
        ps_zT = [b6[:, 0:C], b7[:, 0:C]]
        ps_lg = [bank[0][:, 0:U * X], bank[3][:, 0:U * X]]
        ps_rk = bank[1][:, 0:U * X]
        ps_cnt = bank[2][:, 0:X]
        ps_hT = [bank[2], bank[3]]
        ps_y2 = [bqk[:, 0:C], bqk[:, 512:512 + C]]

        s_const = sem("s_const")
        s_cload = sem("s_cload")
        s_zz = sem("s_zz")
        s_zeroed = sem("s_zeroed")
        s_etab = sem("s_etab")
        s_zero = sem("s_zero")
        s_dve = sem("s_dve")
        s_act = sem("s_act")
        s_ask = sem("s_ask")
        s_xin = sems("s_xin", 2)
        s_xn = sem("s_xn")
        s_xnst = sem("s_xnst")
        s_prep = sem("s_prep")
        s_tr = sem("s_tr")
        s_d = sem("s_d")
        s_msg = sem("s_msg")
        s_evac = sem("s_evac")
        s_idx = sem("s_idx")
        s_gath = sems("s_gath", EB)
        s_scat = sems("s_scat", EB)
        s_xst = sem("s_xst")
        s_xTp = sem("s_xTp")
        s_xT = sem("s_xT")
        s_qkv = sem("s_qkv")
        s_bias = sem("s_bias")
        s_sq = sem("s_sq")
        s_v1 = sem("s_v1")
        s_kk = sem("s_kk")
        s_acc = sem("s_acc")
        s_mom = sem("s_mom")
        s_qd = sem("s_qd")
        s_qtr = sem("s_qtr")
        s_qn = sem("s_qn")
        s_qq = sem("s_qq")
        s_yi = sem("s_yi")
        s_on = sem("s_on")
        s_oTp = sem("s_oTp")
        s_oT = sem("s_oT")
        s_pr = sem("s_pr")
        s_x1 = sem("s_x1")
        s_xr = sems("s_xr", 2)
        s_w = sem("s_w")
        s_accl = sem("s_accl")
        s_bx = sem("s_bx")
        s_z = sem("s_z")
        s_zTp = sem("s_zTp")
        s_zT = sem("s_zT")
        s_lg = sem("s_lg")
        s_cc = sem("s_cc")
        s_rk = sem("s_rk")
        s_idxz = sem("s_idxz")
        s_zsc = [sems(f"s_zsc{k}", U) for k in range(2)]
        s_cnt = sem("s_cnt")
        s_tab = sem("s_tab")
        s_tail = sem("s_tail")
        s_dz = sem("s_dz")
        s_gb = sem("s_gb")
        s_ztin = sems("s_ztin", 4)
        s_b2in = sems("s_b2in", 2)
        s_yst = sems("s_yst", 2)
        f_zT = sem("f_zT")
        f_zTe = sem("f_zTe")
        f_w = sem("f_w")
        f_hT = sem("f_hT")
        f_hTe = sem("f_hTe")
        f_y = sem("f_y")
        f_yo = sem("f_yo")
        s_idxc = sem("s_idxc")
        s_yg = sems("s_yg", 2)
        s_zc = sem("s_zc")
        s_fn = sem("s_fn")
        s_fo = sem("s_fo")
        s_ost = sems("s_ost", 2)

        s_here = sem("s_here")

        NCONST = 21
        NCLOAD = 16 * 8
        LAG = 3
        NZERO = NACC * (NU + 1)
        QI = 9

        block = ctx.enter_context(nc.Block())

        @block.sync
        def _(sp):
            def load_x(i, k):
                u = 2 * i + k
                sp.dma_start(rows[:, ds(u * U, U), :],
                             x[ds(u * U * P, U * P), :].rearrange("(u p) c -> p u c", p=P)).then_inc(s_xin[k], 16)

            def clear(c, u):
                sp.dma_start(acc_dram[c][ds(u * U * P, U * P), :].rearrange("(p r) c -> p (r c)", p=P),
                             zero[:, 0:U * C]).then_inc(s_zeroed, 16)

            load_x(0, 0)
            load_x(0, 1)
            sp.dma_start(srcI[:], srcT.rearrange("p (b j) -> p b j", j=EB)).then_inc(s_etab, 16)
            sp.dma_start(dstI[:], dstT.rearrange("p (b j) -> p b j", j=EB)).then_inc(s_etab, 16)
            sp.dma_start(wE[:], wT.rearrange("p (b j) -> p b j", j=EB)).then_inc(s_etab, 16)
            sp.wait_ge(s_zero, 1)
            with sp.Fori(1, NU // 2) as i:
                for k in range(2):
                    sp.wait_ge(s_xin[k], 16 * i)
                    load_x(i, k)
                    clear(0, 2 * i + k)
            for u in range(2):
                clear(0, u)
            for c in range(NACC):
                sp.dma_start(acc_dram[c][NP:AR, :], zero[:, 0:C]).then_inc(s_zeroed, 16)
            with sp.Fori(0, NU) as u:
                sp.wait_ge(s_xn, u + 1)
                sp.dma_start(xn_dram[ds(u * U * P, U * P), :].rearrange("(u p) c -> p u c", p=P),
                             rows[:, ds(u * U, U), :]).then_inc(s_xnst, 16)
            with sp.Fori(0, NU) as u:
                clear(1, u)
            def load_xr(i, k):
                sp.dma_start(xin[k], x[ds((2 * i + k) * P, P), :]).then_inc(s_xr[k], 16)

            load_xr(0, 0)
            load_xr(0, 1)
            with sp.Fori(1, NT // 2) as i:
                for k in range(2):
                    sp.wait_ge(s_x1, 2 * i + k - 1)
                    load_xr(i, k)
            def load_acc(u):
                for k in range(2):
                    sp.dma_start(accb[:, k], acc_dram[k][ds(u * U * P, U * P), :].rearrange("(u p) c -> p u c", p=P)
                                 ).then_inc(s_accl, 16)

            for a in range(0, 20, U):
                sp.dma_start(z_dram[X * R + a * P:X * R + (a + U) * P, :].rearrange("(p r) c -> p (r c)", p=P),
                             zero).then_inc(s_zz, 16)
            sp.wait_ge(s_zz, 16 * 4)
            for j in range(EB):
                sp.wait_ge(s_scat[j], 16 * NB)
            load_acc(0)
            sp.wait_ge(s_x1, NT)
            sp.wait_ge(s_evac, 4 + 4 * NB)
            for u in range(1, NU):
                if u <= 8:
                    e = 4 * ((u - 1) % 4)
                    if u <= 4:
                        sp.dma_start(w1s[:, e:e + 4], w1[e:e + 4].rearrange("e (c p) f -> p e c f", p=P)).then_inc(s_w, 16)
                    else:
                        sp.dma_start(w2s[:, e:e + 4], w2[e:e + 4].rearrange("e (c p) f -> p e c f", p=P)).then_inc(s_w, 16)
                sp.wait_ge(s_bx, u)
                load_acc(u)
            sp.wait_ge(s_dz, 3)
            sp.wait_ge(s_tab, 1)
            with sp.Fori(0, X // 2) as e:
                row = sp.value_load(tailI[0:1, ds(e, 1)], min_val=0, max_val=X * R - P)
                sp.dma_start(z_dram[ds(row, P), :], zeros).then_inc(s_tail, 16)
            for k in range(2):
                for j in range(U):
                    sp.wait_ge(s_zsc[k][j], 32 * (NU // 2))
            sp.wait_ge(s_tail, 16 * X)
            sp.wait_ge(s_tab, 2)

            def load_z(t, k):
                row = sp.value_load(rowI[0:1, ds(t, 1)], min_val=0, max_val=ZR - P)
                sp.dma_start(zt[k], z_dram[ds(row, P), :]).then_inc(s_ztin[k], 16)

            def load_b2(t, k):
                ex = sp.value_load(expI[0:1, ds(t, 1)], min_val=0, max_val=X - 1)
                sp.dma_start(b2t[k], bass.AP(tensor=b2.tensor, offset=b2.offset + ex * C, ap=[[0, P], [1, C]])).then_inc(s_b2in[k], 16)

            for k in range(4):
                load_z(k, k)
            for k in range(2):
                load_b2(k, k)
            with sp.Fori(0, FT // 4) as i:
                for k in range(4):
                    t = 4 * i + k
                    sp.wait_ge(f_zT, t + 1)
                    load_z(t + 4, k)
                    sp.wait_ge(f_yo, t + 3)
                    sp.dma_start(y_dram[ds(t * P, P), :], yo[k % 2]).then_inc(s_yst[k % 2], 16)
                    load_b2(t + 2, k % 2)
            for k in range(4):
                sp.wait_ge(s_ztin[k], 16 * (FT // 4 + 1))
            for k in range(2):
                sp.wait_ge(s_yst[k], 16 * (FT // 2))
                sp.wait_ge(s_b2in[k], 16 * (FT // 2 + 1))
            sp.dma_start(gamma_b, gamma.partition_broadcast(P)).then_inc(s_gb, 16)
            sp.dma_start(beta_b, beta.partition_broadcast(P)).then_inc(s_gb, 16)
            sp.sem_inc(s_tail, 1)
            with sp.Fori(0, NU // 2) as i:
                for k in range(2):
                    u = 2 * i + k
                    sp.wait_ge(s_fo, u + 1)
                    sp.dma_start(out[ds(u * U * P, U * P), :].rearrange("(u p) c -> p u c", p=P),
                                 fc[k]).then_inc(s_ost[k], 16)
            for k in range(2):
                sp.wait_ge(s_ost[k], 16 * (NU // 2))

        @block.gpsimd
        def _(pool):
            n = [0]

            def done(ins):
                n[0] += 1
                ins.then_inc(s_const, 1)

            def masked(t, pattern, op, base, cm, fill, also=None):
                pool.wait_ge(s_const, n[0])
                done(pool.affine_select(out=t, in_=t, pattern=pattern, compare_op=op, fill=fill, base=base,
                                        channel_multiplier=cm))

            done(pool.memset(eps[:], EPS_LN))
            pool.memset(zero, 0.0).then_inc(s_zero, 1)
            done(pool.memset(ident[:], 0.0))
            done(pool.memset(upper[:], 1.0))
            done(pool.memset(lower, 1.0))
            done(pool.memset(ones[:], 1.0))
            done(pool.memset(mask_l, 1.0))
            done(pool.memset(mask_s, 1.0))
            done(pool.memset(half0, 1.0))
            done(pool.memset(rscale, 1.0 / N))
            done(pool.iota(iota16[:], [[1, X]], base=0, channel_multiplier=0, allow_small_or_imprecise_dtypes=True))
            done(pool.iota(base16[:], [[R, X]], base=0, channel_multiplier=0, allow_small_or_imprecise_dtypes=True))
            done(pool.iota(dummy, [[0, 1]], base=NP, channel_multiplier=1, allow_small_or_imprecise_dtypes=True))
            masked(ident[:], [[-1, P]], ALU.not_equal, 0, 1, 1.0)
            masked(upper[:], [[1, P]], ALU.is_gt, 0, -1, 0.0)
            masked(lower, [[-1, P]], ALU.is_gt, 0, 1, 0.0)
            masked(mask_l, [[-D, 4], [0, VH]], ALU.is_ge, 0, 1, 0.0)
            masked(mask_l, [[D, 4], [0, VH]], ALU.is_ge, D - 1, -1, 0.0)
            masked(mask_s, [[-16, H], [0, VH]], ALU.is_ge, 0, 1, 0.0)
            masked(mask_s, [[16, H], [0, VH]], ALU.is_ge, 15, -1, 0.0)
            masked(half0, [[0, 1]], ALU.is_ge, -D, 1, 0.5)
            masked(rscale, [[-P, NT]], ALU.is_ge, N - 1, -1, 0.0)
            assert n[0] == NCONST

            def gather(b, j, k):
                pool.wait_ge(s_msg, EB * b + j + 1)
                pool.sem_inc(s_here, 1)
                pool.indirect_dma_start(out=gx[j], out_offset=None, in_=xn_dram,
                                        in_offset=bass.IndirectOffsetOnAxis(ap=dstb[k][:, j:j + 1], axis=0)
                                        ).then_inc(s_gath[j], 16)

            def scatter(b, j, k, first=False):
                pool.wait_ge(s_evac, 4 * b + j // 2 + 5)
                if j >= 2:
                    pool.wait_ge(s_scat[j - 2], 16 * b + 16)
                elif not first:
                    pool.wait_ge(s_scat[j + 6], 16 * b)
                pool.sem_inc(s_here, 1)
                pool.indirect_dma_start(out=acc_dram[j % 2], in_=msg[:, j, :],
                                        out_offset=bass.IndirectOffsetOnAxis(ap=idxb[k][:, j:j + 1], axis=0),
                                        in_offset=None, compute_op=ALU.add).then_inc(s_scat[j], 16)

            def turn(b, k, first=False):
                pool.wait_ge(s_prep, b + 2)
                for j in range(EB):
                    gather(b + 1, j, 1 - k)
                    if j >= LAG:
                        if j == LAG:
                            pool.wait_ge(s_idx, b + 1)
                        scatter(b, j - LAG, k, first)
                    elif not first:
                        scatter(b - 1, j - LAG + EB, 1 - k)

            pool.wait_ge(s_xnst, 16 * NU)
            pool.wait_ge(s_prep, 1)
            for j in range(EB):
                gather(0, j, 0)
            pool.wait_ge(s_zeroed, 16 * NZERO)
            turn(0, 0, first=True)
            turn(1, 1)
            with pool.Fori(1, NB // 2 - 1) as i:
                turn(2 * i, 0)
                turn(2 * i + 1, 1)
            turn(NB - 2, 0)
            for j in range(EB - LAG, EB):
                scatter(NB - 2, j, 0)
            pool.wait_ge(s_idx, NB)
            for j in range(EB):
                scatter(NB - 1, j, 1)

            def scatter_z(u, k):
                pool.wait_ge(s_idxz, u + 1)
                pool.sem_inc(s_here, 1)
                for j in range(U):
                    for m in range(2):
                        pool.indirect_dma_start(out=z_dram, in_=zt5[k][:, j, :], in_offset=None,
                                                out_offset=bass.IndirectOffsetOnAxis(ap=idxz[k][:, j, m:m + 1], axis=0)
                                                ).then_inc(s_zsc[k][j], 16)

            pool.wait_ge(s_zz, 16 * 4)
            with pool.Fori(0, NU // 2 - 1) as i:
                for k in range(2):
                    scatter_z(2 * i + k, k)
            scatter_z(NU - 2, 0)
            pool.wait_ge(s_bx, NU)
            pool.memset(zeros, 0.0).then_inc(s_dz, 1)
            pool.iota(thr, [[P, NT]], base=0, channel_multiplier=0, allow_small_or_imprecise_dtypes=True).then_inc(s_dz, 1)
            pool.iota(tau, [[1, FTL]], base=0, channel_multiplier=0, allow_small_or_imprecise_dtypes=True).then_inc(s_dz, 1)
            scatter_z(NU - 1, 1)
            pool.wait_ge(s_tail, 16 * X + 1)
            with pool.Fori(0, NU // 2) as i:
                for k in range(2):
                    pool.wait_ge(s_idxc, 2 * i + k + 1)
                    pool.sem_inc(s_here, 1)
                    for j in range(U):
                        for m in range(2):
                            pool.indirect_dma_start(out=yg[k][:, m, j, :], out_offset=None, in_=y_dram,
                                                    in_offset=bass.IndirectOffsetOnAxis(ap=idxz[k][:, j, m:m + 1], axis=0)
                                                    ).then_inc(s_yg[k], 16)

        @block.scalar
        def _(act):
            act.dma_start(wqkv, wqkvT.rearrange("(c p) n -> p c n", p=P)).then_inc(s_cload, 16)
            act.dma_start(wproj, wprojT.rearrange("(c p) n -> p c n", p=P)).then_inc(s_cload, 16)
            act.dma_start(bqkv_b, bqkv.partition_broadcast(P)).then_inc(s_cload, 16)
            act.dma_start(bproj_b, bproj.partition_broadcast(P)).then_inc(s_cload, 16)
            act.dma_start(temp_b, temp.partition_broadcast(P)).then_inc(s_cload, 16)
            act.dma_start(gb_b[:], gate_b.partition_broadcast(P)).then_inc(s_cload, 16)
            act.dma_start(gw[:], gate_w.rearrange("(c p) n -> p c n", p=P)).then_inc(s_cload, 16)
            act.dma_start(b1c[:], b1T).then_inc(s_cload, 16)
            act.sem_inc(s_evac, 4)
            act.sem_inc(s_qq, 3)
            act.sem_inc(f_zTe, 2)
            act.sem_inc(f_hTe, 2)
            act.wait_ge(s_const, 1)

            def answer(q, out_, in_, func, **kw):
                act.wait_ge(s_ask, q + 1)
                act.activation(out_, in_, func, **kw).then_inc(s_act, 1)

            NORM_ASKS = 2 * NU

            def unit_root(u, q):
                answer(q, std5[:], mv[:, ds(u * U, U), 1:2].rearrange("p u o -> p (u o)"), ACT.Sqrt, bias=eps[:])

            def norm_rows(u):
                act.wait_ge(s_ask, 2 * u + 2)
                for j in range(U):
                    t = u * U + j
                    row = rows[:, ds(t, 1), :].rearrange("p o c -> p (o c)")
                    a = act.activation(row, row, ACT.Identity, scale=rstd[:, ds(t, 1)], bias=nbias[:, ds(t, 1)])
                a.then_inc(s_xn, 1)

            unit_root(0, 0)
            with act.Fori(0, NU - 1) as u:
                norm_rows(u)
                unit_root(u + 1, 2 * u + 2)
            norm_rows(NU - 1)
            act.wait_ge(s_const, NCONST)
            act.wait_ge(s_cload, NCLOAD)

            def evac(b, q):
                act.wait_ge(s_msg, EB * b + 2 * q + 2 + EB)
                if not (isinstance(b, int) and b == 0):
                    for j in (2 * q, 2 * q + 1):
                        act.wait_ge(s_scat[j], 16 * b)
                act.activation(msg[:, 2 * q:2 * q + 2, :], ps_msg, ACT.Copy).then_inc(s_evac, 1)

            def still_xn(s, k):
                act.activation(xst[k], rows[:, ds(s, 1), :].rearrange("p o c -> p (o c)"), ACT.Copy).then_inc(s_xst, 1)

            def evac_xT(s, k):
                act.wait_ge(s_xTp, s + 1)
                act.activation(xT[k], ps_xT.rearrange("p (c n) -> p c n", c=2), ACT.Copy).then_inc(s_xT, 1)

            def key_turn(s, k, last=False):
                if not last:
                    still_xn(s + 1, 1 - k)
                act.wait_ge(s_bias, s + 2)
                act.activation(sq, qkvb[:, 0:2 * C], ACT.Square).then_inc(s_sq, 1)
                answer(NORM_ASKS + s, nrm, ss, ACT.Sqrt)
                act.wait_ge(s_acc, s + 1)
                act.activation(v1[k][:, :, 1:VH], qkvb[:, 2 * C:3 * C].rearrange("p (h d) -> p h d", h=H), ACT.Copy,
                               scale=rscale[:, ds(s, 1)])
                act.activation(v1[k][:, :, 0:1], ones[:, 0:H].unsqueeze(2), ACT.Copy,
                               scale=rscale[:, ds(s, 1)]).then_inc(s_v1, 1)
                evac(s, 0)
                if not last:
                    evac_xT(s + 1, 1 - k)
                for q in range(1, 4):
                    evac(s, q)

            act.wait_ge(s_xn, NU)
            still_xn(0, 0)
            evac_xT(0, 0)
            key_turn(0, 0)
            key_turn(1, 1)
            with act.Fori(1, NT // 2 - 1) as i:
                key_turn(2 * i, 0)
                key_turn(2 * i + 1, 1)
            key_turn(NT - 2, 0)
            key_turn(NT - 1, 1, last=True)

            def repeat_q(s, k):
                q = rows[:, ds(s, 1), :].rearrange("p o (h d) -> p (o h) d", h=H)
                act.activation(kd[k][:, :, 0:D], q, ACT.Copy)
                act.activation(kd[k][:, :, D:DW], q[:, :, 0:16], ACT.Copy)
                act.activation(kc[k].rearrange("p (h d) -> p h d", h=H), q, ACT.Copy).then_inc(s_qd, 1)

            def query_turn(s, k, last=False):
                for m in range(QI):
                    act.wait_ge(s_qtr, QI * s + m + 1)
                    act.wait_ge(s_yi, QI * s + m + 1)
                    w = 3 if m == 0 else KC
                    act.activation(qq[m % 3][:, 0:w, :], bank[m % 3][:, 0:w * P].rearrange("p (g n) -> p g n", g=w),
                                   ACT.Copy).then_inc(s_qq, 1)
                    if m == 1 and not last:
                        repeat_q(s + 1, 1 - k)
                    if m == 4 and not last:
                        evac(NT + 1 + s, 0)
                    if m == 7 and not last:
                        evac(NT + 1 + s, 1)
                if not last:
                    evac(NT + 1 + s, 2)
                act.wait_ge(s_oTp, s + 1)
                act.activation(oT[k], ps_oT.rearrange("p (c n) -> p c n", c=2), ACT.Copy).then_inc(s_oT, 1)
                if not last:
                    evac(NT + 1 + s, 3)

            evac(NT, 0)
            evac(NT, 1)
            act.wait_ge(s_mom, 1)
            repeat_q(0, 0)
            evac(NT, 2)
            evac(NT, 3)
            with act.Fori(0, NT // 2 - 1) as i:
                query_turn(2 * i, 0)
                query_turn(2 * i + 1, 1)
            query_turn(NT - 2, 0)
            query_turn(NT - 1, 1, last=True)

            def gate_root(u):
                unit_root(u, NORM_ASKS + NT + 2 * u)

            def gate_z(u, k, i):
                act.wait_ge(s_ask, NORM_ASKS + NT + 2 * u + 2)
                for j in range(U):
                    t = u * U + j
                    if not (isinstance(i, int) and i == 0):
                        act.wait_ge(s_zsc[k][j], 32 * i)
                    act.activation(zt5[k][:, j, :], rows[:, ds(t, 1), :].rearrange("p o c -> p (o c)"), ACT.Identity,
                                   scale=rstd[:, ds(t, 1)], bias=nbias[:, ds(t, 1)]).then_inc(s_z, 1)
                for j in range(U):
                    g = (U * k + j) % 2
                    act.wait_ge(s_zTp, u * U + j + 1)
                    act.activation(zT[g][:], ps_zT[g].rearrange("p (c n) -> p c n", c=2), ACT.Copy).then_inc(s_zT, 1)

            for k in range(2):
                gate_root(k)
                gate_z(k, k, 0)
            with act.Fori(1, NU // 2) as i:
                for k in range(2):
                    gate_root(2 * i + k)
                    gate_z(2 * i + k, k, i)
            act.wait_ge(s_dz, 3)
            act.wait_ge(s_tab, 1)
            with act.Fori(X // 2, X) as e:
                row = act.value_load(tailI[0:1, ds(e, 1)], min_val=0, max_val=X * R - P)
                act.dma_start(z_dram[ds(row, P), :], zeros).then_inc(s_tail, 16)
            nq = NORM_ASKS + NT + 2 * NU

            def evac_zT(t, k):
                act.wait_ge(f_zT, t + 1)
                act.activation(zT[k % 2][:], ps_zT[k % 2].rearrange("p (c n) -> p c n", c=2), ACT.Copy).then_inc(f_zTe, 1)

            evac_zT(0, 0)
            evac_zT(1, 1)
            act.wait_ge(s_ask, nq + 1)
            act.activation(topv[:, :, 1], topv[:, :, 1], ACT.Exp).then_inc(s_act, 1)
            act.wait_ge(s_tab, 3)
            with act.Fori(0, FT // 4) as i:
                for k in range(4):
                    t = 4 * i + k
                    ex = act.value_load(expI[0:1, ds(t, 1)], min_val=0, max_val=X - 1)
                    act.wait_ge(f_hT, t + 1)
                    for c in range(FC):
                        a = act.activation(hT[k % 2][:, c, :], ps_hT[k % 2][:, c * P:(c + 1) * P], ACT.Relu,
                                           bias=b1c[:, ds(ex * FC + c, 1)])
                    a.then_inc(f_hTe, 1)
                    evac_zT(t + 2, k)

            def combine_z(u, k):
                for j in range(U):
                    t = u * U + j
                    a = act.activation(zc[k][:, j, :], rows[:, ds(t, 1), :].rearrange("p o c -> p (o c)"), ACT.Identity,
                                       scale=rstd[:, ds(t, 1)], bias=nbias[:, ds(t, 1)])
                a.then_inc(s_zc, 1)

            def combine_root(u):
                answer(nq + 2 + 2 * u, std5[:], mv5[:, :, 1], ACT.Sqrt, bias=eps[:])

            def combine_rows(u, k):
                act.wait_ge(s_ask, nq + 4 + 2 * u)
                for j in range(U):
                    a = act.activation(fn[k][:, j, :], zc[k][:, j, :], ACT.Identity, scale=rc[:, j:j + 1],
                                       bias=nc5[:, j:j + 1])
                a.then_inc(s_fn, 1)

            act.wait_ge(s_ask, nq + 2)
            combine_z(0, 0)
            combine_z(1, 1)
            combine_root(0)
            with act.Fori(0, NU // 2 - 1) as i:
                for k in range(2):
                    u = 2 * i + k
                    combine_rows(u, k)
                    act.wait_ge(s_fn, u + 1)
                    combine_z(u + 2, k)
                    combine_root(u + 1)
            combine_rows(NU - 2, 0)
            combine_root(NU - 1)
            combine_rows(NU - 1, 1)

        @block.vector
        def _(v):
            n = [0]
            base = [0]

            def mark(ins):
                n[0] += 1
                ins.then_inc(s_dve, 1)

            def join():
                v.wait_ge(s_dve, base[0] + n[0])

            def link(ins):
                mark(ins)
                join()

            def loop(first, last, body):
                start = base[0] + n[0]
                per = body_steps[body]
                with v.Fori(first, last) as i:
                    base[0], n[0] = start + (i - first) * per, 0
                    body(i, False)
                    assert n[0] == per, n[0]
                base[0], n[0] = start + (last - first) * per, 0

            def flat(a):
                return a.rearrange("p o c -> p (o c)")

            def tile(t):
                return flat(rows[:, ds(t, 1), :])

            v.sem_inc(s_d, 4)
            v.sem_inc(s_bias, 1)
            v.sem_inc(f_yo, 2)

            def row_stats(row, mv_of=None):
                for j in range(U):
                    mark(v.bn_stats(st[:, j, :], row(j)))
                join()
                v.sem_inc(s_here, 1)
                for j in range(U):
                    mark(v.bn_aggr(mv5[:, j, :], st[:, j, :]))
                join()
                if mv_of is not None:
                    link(v.tensor_copy(mv_of, mv5[:]))

            def row_scales(mean, r, b, q):
                v.wait_ge(s_act, q + 1)
                link(v.reciprocal(r, std5[:]))
                link(v.scalar_tensor_tensor(out=b, in0=mean, scalar=-1.0, in1=r, op0=ALU.mult, op1=ALU.mult))

            def unit_scales(u, q):
                cols = ds(u * U, U)
                row_scales(mv[:, cols, 0:1].rearrange("p u o -> p (u o)"), rstd[:, cols], nbias[:, cols], q)
                v.sem_inc(s_ask, 1)

            def norm_stats(u, i, k):
                v.wait_ge(s_xin[k], 16 * (i + 1))
                row_stats(lambda j: tile(u * U + j), mv[:, ds(u * U, U), :])

            def norm_pair(i, first):
                last = isinstance(i, int) and i == NU // 2 - 1
                norm_stats(2 * i + 1, i, 1)
                unit_scales(2 * i, 2 * i)
                v.sem_inc(s_ask, 1)
                if not last:
                    norm_stats(2 * i + 2, i + 1, 0)
                unit_scales(2 * i + 1, 2 * i + 1)
                if not last:
                    v.sem_inc(s_ask, 1)

            def prep(b, k):
                if not (isinstance(b, int) and b == 0):
                    v.wait_ge(s_msg, EB * b)
                if not (isinstance(b, int) and b < 2):
                    v.wait_ge(s_idx, b - 1)
                mark(v.tensor_copy(srcb[k], flat(srcI[:, ds(b, 1), :])))
                mark(v.tensor_copy(wb[k], flat(wE[:, ds(b, 1), :])))
                v.tensor_copy(dstb[k][:], flat(dstI[:, ds(b, 1), :])).then_inc(s_prep, 1)

            def equal(b, j, k):
                if j % 4 == 0:
                    v.wait_ge(s_tr, 2 * b + j // 4 + 1)
                v.wait_ge(s_msg, EB * b + j + 1)
                v.wait_ge(s_d, EB * b + j + 1)
                v.tensor_scalar(wd[j], ps_src[:, j % 4, :], srcb[k][:, j:j + 1], wb[k][:, j:j + 1],
                                ALU.is_equal, ALU.mult)
                v.scalar_tensor_tensor(out=junk[j % 4], in0=ps_src[:, j % 4, :], scalar=srcb[k][:, j:j + 1], in1=lower,
                                       op0=ALU.is_equal, op1=ALU.mult, accum_out=cnt[:, j:j + 1]).then_inc(s_d, 1)

            def scatter_rows(b, k):
                v.wait_ge(s_d, EB * b + EB + 4)
                link(v.tensor_scalar(dup, cnt, 1.0, None, ALU.min))
                link(v.tensor_scalar(ddd, srcb[k], dummy[:, 0:1], -1.0, ALU.subtract, ALU.mult))
                link(v.tensor_tensor(ddd, ddd, dup, ALU.mult))
                v.wait_ge(s_evac, 4 * b + 4)
                v.tensor_tensor(idxb[k][:], srcb[k], ddd, ALU.add).then_inc(s_idx, 1)

            def shifted(k, h):
                return v.tensor_tensor(kk[k][:, h], window(kd[k], h * DW, [[0, 16], [1, D]]),
                                       window(kd[k], h * DW, [[1, 16], [1, D]]), ALU.mult)

            def shift16(k):
                return v.tensor_tensor(k16[k].rearrange("p (h i) -> p h i", h=H), kd[k][:, :, 0:16], kd[k][:, :, 16:32],
                                       ALU.mult)

            def key_pair(i, first):
                for k in range(2):
                    s = 2 * i + k
                    v.wait_ge(s_qkv, s + 1)
                    if not (first and k == 0):
                        v.wait_ge(s_v1, s)
                        v.wait_ge(s_kk, s)
                    v.tensor_tensor(qkvb, bqk[:, 0:3 * C], bqkv_b, ALU.add).then_inc(s_bias, 1)
                    for j in range(4):
                        equal(s, j, k)
                    v.wait_ge(s_sq, s + 1)
                    link(v.tensor_reduce(ss, sq.rearrange("p (g d) -> p g d", d=D), AX.X, ALU.add))
                    link(v.scalar_tensor_tensor(out=ss, in0=ss, scalar=1e-30, in1=ssc, op0=ALU.max, op1=ALU.mult))
                    v.sem_inc(s_ask, 1)
                    prep(s + 1, 1 - k)
                    for j in range(4, EB):
                        equal(s, j, k)
                    scatter_rows(s, k)
                    v.wait_ge(s_act, NU + s + 1)
                    link(v.tensor_scalar(nrm, nrm, EPS_N, None, ALU.max))
                    link(v.reciprocal(rn, nrm))
                    link(v.tensor_tensor(rn, rn, fac, ALU.mult))
                    qh = qkvb[:, 0:C].rearrange("p (h d) -> p h d", h=H)
                    kh = qkvb[:, C:2 * C].rearrange("p (h d) -> p h d", h=H)
                    rq = rn[:, 0:H].unsqueeze(2)
                    rk_ = rn[:, H:2 * H].unsqueeze(2)
                    v.wait_ge(s_acc, s + 1)
                    mark(v.tensor_tensor(kc[k].rearrange("p (h d) -> p h d", h=H), kh, rk_.broadcast_to([P, H, D]), ALU.mult))
                    mark(v.tensor_tensor(kd[k][:, :, 0:D], kh, rk_.broadcast_to([P, H, D]), ALU.mult))
                    link(v.tensor_tensor(kd[k][:, :, D:DW], kh[:, :, 0:16], rk_.broadcast_to([P, H, 16]), ALU.mult))
                    if first and k == 0:
                        v.wait_ge(s_xnst, 16 * NU)
                    v.tensor_tensor(tile(s).rearrange("p (h d) -> p h d", h=H), qh, rq.broadcast_to([P, H, D]), ALU.mult)
                    for h in range(H):
                        shifted(k, h)
                    shift16(k).then_inc(s_kk, 1)
                    join()

            def edge_block(b, k):
                for j in range(4):
                    equal(b, j, k)
                prep(b + 1, 1 - k)
                for j in range(4, EB):
                    equal(b, j, k)
                scatter_rows(b, k)

            def query_pair(i, first):
                for k in range(2):
                    s = 2 * i + k
                    last = isinstance(s, int) and s == NT - 1

                    def next_heads(a, b):
                        if not last:
                            for h in range(a, b):
                                shifted(1 - k, h).then_inc(s_qn, 1)

                    if not last:
                        edge_block(NT + 1 + s, 1 - k)
                    if not last:
                        v.wait_ge(s_qd, s + 2)
                        shift16(1 - k).then_inc(s_qn, 1)
                    next_heads(0, 5)
                    v.wait_ge(s_yi, QI * s + QI + 3)
                    link(v.tensor_tensor(yb.rearrange("p h e -> p (h e)"), ps_y, m0, ALU.add))
                    link(v.reciprocal(yr, yb[:, :, 0]))
                    v.tensor_tensor(on[k].rearrange("p (h d) -> p h d", h=H), yb[:, :, 1:VH],
                                    yr.unsqueeze(2).broadcast_to([P, H, D]), ALU.mult).then_inc(s_on, 1)
                    next_heads(5, 7)
                    v.wait_ge(s_pr, s + 1)
                    v.wait_ge(s_xr[k], 16 * (i + 1))
                    link(v.tensor_tensor(pr, ps_pr, bproj_b, ALU.add))
                    v.tensor_tensor(tile(s), pr, xin[k], ALU.add).then_inc(s_x1, 1)
                    next_heads(7, 8)

            def gate_sum(u):
                mine = rows[:, ds(u * U, U), :]
                v.wait_ge(s_accl, 32 * (u + 1))
                link(v.tensor_tensor(mine, mine, accb[:, 0], ALU.add))
                link(v.tensor_tensor(mine, mine, accb[:, 1], ALU.add))
                v.sem_inc(s_bx, 1)

            def gate_front(u):
                row_stats(lambda j: tile(u * U + j), mv[:, ds(u * U, U), :])
                v.sem_inc(s_ask, 1)

            def gate_back(u, k, i, first, more):
                v.wait_ge(s_lg, u + 1)
                link(v.tensor_tensor(lg[:], ps_lg[k].rearrange("p (u e) -> p u e", u=U),
                                     gb_b[:].unsqueeze(1).broadcast_to([P, U, X]), ALU.add))
                v.sem_inc(s_here, 1)
                for j in range(U):
                    mark(v.max(m8[:, j, :], lg[:, j, :]))
                join()
                v.sem_inc(s_here, 1)
                for j in range(U):
                    mark(v.max_index(i8[:, j, :], m8[:, j, :], lg[:, j, :]))
                mark(v.tensor_copy(topv[:, ds(u * U, U), :], m8[:, :, 0:2]))
                join()
                link(v.tensor_copy(idf[:], i8[:, :, 0:2]))
                for m in range(2):
                    mark(v.tensor_tensor(oh[m], iota16[:].unsqueeze(1).broadcast_to([P, U, X]),
                                         idf[:, :, m:m + 1].broadcast_to([P, U, X]), ALU.is_equal))
                join()
                link(v.tensor_tensor(cc, oh[0], oh[1], ALU.add))
                v.sem_inc(s_cc, 1)
                mark(v.tensor_reduce(csum[:], cc.rearrange("p u e -> p e u"), AX.X, ALU.add))
                if not (isinstance(u, int) and u == NU - 1):
                    unit_scales(u + 1, NU + NT + u + 1)
                if more:
                    gate_sum(u + 2)
                v.wait_ge(s_rk, u + 1)
                join()
                mark(v.tensor_tensor(crun[:], crun[:], csum[:], ALU.add))
                link(v.tensor_tensor(rk, ps_rk.rearrange("p (u e) -> p u e", u=U),
                                     base16[:].unsqueeze(1).broadcast_to([P, U, X]), ALU.add))
                for m in range(2):
                    link(v.tensor_tensor(pk, rk, oh[m], ALU.mult))
                    link(v.tensor_reduce(posf[:, :, m:m + 1], pk, AX.X, ALU.add))
                if not first:
                    for j in range(U):
                        v.wait_ge(s_zsc[k][j], 32 * i)
                v.tensor_copy(idxz[k][:], posf[:]).then_inc(s_idxz, 1)
                mark(v.tensor_copy(posT[:, ds(u * U, U), :], posf[:]))
                mark(v.tensor_copy(expT[:, ds(u * U, U), :], idf[:]))

            def gate_pair(i, first):
                for k in range(2):
                    u = 2 * i + k
                    if not (isinstance(u, int) and u == NU - 1):
                        gate_front(u + 1)
                    gate_back(u, k, i, first, more=not (isinstance(i, int) and i == NU // 2 - 1))

            def combine_front(u, i, k, more=True):
                v.wait_ge(s_yg[k], 160 * (i + 1))
                v.wait_ge(s_zc, u + 1)
                for m in range(2):
                    for j in range(U):
                        mark(v.scalar_tensor_tensor(out=zc[k][:, j, :], in0=yg[k][:, m, j, :],
                                                    scalar=flat(topv[:, ds(u * U + j, 1), m:m + 1]),
                                                    in1=zc[k][:, j, :], op0=ALU.mult, op1=ALU.add))
                    join()
                if more:
                    v.tensor_copy(idxz[k][:], posT[:, ds((u + 2) * U, U), :]).then_inc(s_idxc, 1)
                row_stats(lambda j: zc[k][:, j, :])
                v.sem_inc(s_ask, 1)

            def combine_scales(u):
                row_scales(mv5[:, :, 0], rc, nc5, NU + NT + NU + 1 + u)
                v.sem_inc(s_ask, 1)

            def combine_gamma(u, k):
                v.wait_ge(s_fn, u + 1)
                link(v.tensor_tensor(fn[k], fn[k], gamma_b.unsqueeze(1).broadcast_to([P, U, C]), ALU.mult))

            def combine_out(u, i, k, first):
                if not first:
                    v.wait_ge(s_ost[k], 16 * i)
                link(v.tensor_tensor(fc[k], fn[k], beta_b.unsqueeze(1).broadcast_to([P, U, C]), ALU.add))
                v.tensor_tensor(fc[k], fc[k], rows[:, ds(u * U, U), :], ALU.add).then_inc(s_fo, 1)

            def combine_pair(i, first, last=False):
                combine_front(2 * i + 1, i, 1, more=not last)
                combine_gamma(2 * i, 0)
                combine_scales(2 * i + 1)
                combine_out(2 * i, i, 0, first)
                if not last:
                    combine_front(2 * i + 2, i + 1, 0, more=not (isinstance(i, int) and i == NU // 2 - 2))
                combine_gamma(2 * i + 1, 1)
                if not last:
                    combine_scales(2 * i + 2)
                combine_out(2 * i + 1, i, 1, first)

            body_steps = {
                norm_pair: 2 * (2 * U + 3),
                key_pair: 2 * (2 + 3 + 3 + 3 + 2),
                query_pair: 2 * (2 + 3 + 2 + 1),
                gate_pair: 2 * (2 + 2 * U + 2 + 1 + 1 + U + U + 1 + 1 + 2 + 1 + 1 + 2 + 4 + 2),
                combine_pair: 2 * (2 + 4 * U + 2),
            }

            norm_stats(0, 0, 0)
            v.sem_inc(s_ask, 1)
            loop(0, NU // 2 - 1, norm_pair)
            norm_pair(NU // 2 - 1, False)
            v.wait_ge(s_cload, NCLOAD)
            v.wait_ge(s_const, NCONST)
            mark(v.tensor_scalar(fac[:, 0:H], temp_b, SCALE * SCALE, None, ALU.mult))
            mark(v.memset(fac[:, H:2 * H], SCALE))
            mark(v.memset(ssc[:, 0:H], SCALE * SCALE))
            mark(v.memset(ssc[:, H:2 * H], 1.0))
            mark(v.memset(crun[:], 0.0))
            v.wait_ge(s_etab, 48)
            prep(0, 0)
            join()
            key_pair(0, True)
            loop(1, NT // 2, key_pair)

            edge_block(NT, 0)

            v.wait_ge(s_acc, NT + 2)
            mark(v.tensor_copy(m2[:, 0:15, :], bank[0][:, 0:15 * VH].rearrange("p (c e) -> p c e", e=VH)))
            mark(v.tensor_copy(m2[:, 15:30, :], bank[1][:, 0:15 * VH].rearrange("p (c e) -> p c e", e=VH)))
            mark(v.tensor_copy(m2[:, 30:32, :], bank[2][:, 0:2 * VH].rearrange("p (c e) -> p c e", e=VH)))
            for g in range(2):
                mark(v.scalar_tensor_tensor(out=m1[:, g, :], in0=sum_k[g], scalar=SCALE ** 2,
                                            in1=mask_l.rearrange("p a b -> p (a b)"), op0=ALU.mult, op1=ALU.mult))
                mark(v.tensor_tensor(m16[:, W4 * g:W4 * (g + 1)], sum_16[g],
                                     mask_s.rearrange("p a b -> p (a b)")[:, W4 * g:W4 * (g + 1)], ALU.mult))
                mark(v.tensor_scalar(m0[:, W4 * g:W4 * (g + 1)], sum_v[g], SCALE ** 4, None, ALU.mult))
            join()
            shift0 = m2.rearrange("p (h g) e -> p h g e", g=KC)[:, :, 0, :]
            link(v.tensor_scalar(shift0, shift0, half0[:, 0:1], None, ALU.mult))
            v.sem_inc(s_mom, 1)
            v.wait_ge(s_qd, 1)
            shift16(0).then_inc(s_qn, 1)
            for h in range(H):
                shifted(0, h).then_inc(s_qn, 1)
            loop(0, NT // 2 - 1, query_pair)
            query_pair(NT // 2 - 1, False)
            gate_sum(0)
            gate_front(0)
            unit_scales(0, NU + NT)
            gate_sum(1)
            gate_pair(0, True)
            loop(1, NU // 2 - 1, gate_pair)
            gate_pair(NU // 2 - 1, False)

            join()
            v.sem_inc(s_cc, 1)
            v.wait_ge(s_cnt, 1)
            v.wait_ge(s_dz, 3)
            link(v.tensor_copy(cntR[:], ps_cnt))
            link(v.tensor_tensor(tailI[:], cntR[0:1, :], base16[0:1, :], ALU.add))
            v.sem_inc(s_tab, 1)
            link(v.tensor_tensor(cmpc, cntR[:].unsqueeze(2).broadcast_to([P, X, NT]),
                                 thr.unsqueeze(1).broadcast_to([P, X, NT]), ALU.is_gt))
            link(v.tensor_reduce(ntl, cmpc, AX.X, ALU.add))
            link(v.tensor_tensor_scan(endt, ones[:, 0:X], ntl, 0.0, ALU.mult, ALU.add))
            link(v.tensor_tensor(cmpt, endt[0:1, :].unsqueeze(1).broadcast_to([1, FTL, X]),
                                 tau.unsqueeze(2).broadcast_to([1, FTL, X]), ALU.is_le))
            link(v.tensor_reduce(etau, cmpt, AX.X, ALU.add))
            link(v.tensor_tensor(cmpt, cmpt, ntl[0:1, :].unsqueeze(1).broadcast_to([1, FTL, X]), ALU.mult))
            link(v.tensor_reduce(stau, cmpt, AX.X, ALU.add))
            link(v.tensor_tensor(stau, tau, stau, ALU.subtract))
            mark(v.tensor_scalar(expI, etau, float(X - 1), None, ALU.min))
            link(v.tensor_scalar(etau, etau, float(R), None, ALU.mult))
            link(v.scalar_tensor_tensor(out=rowI, in0=stau, scalar=float(P), in1=etau, op0=ALU.mult, op1=ALU.add))
            v.sem_inc(s_tab, 1)
            for k in range(2):
                for j in range(U):
                    v.wait_ge(s_zsc[k][j], 32 * (NU // 2))
            link(v.tensor_tensor(shift, endt, ntl, ALU.subtract))
            link(v.scalar_tensor_tensor(out=shift, in0=shift, scalar=float(P), in1=base16[:], op0=ALU.mult, op1=ALU.subtract))
            link(v.tensor_tensor(cmpy, expT[:].rearrange("p t k -> p (t k)").unsqueeze(2).broadcast_to([P, 2 * NT, X]),
                                 iota16[:].unsqueeze(1).broadcast_to([P, 2 * NT, X]), ALU.is_equal))
            link(v.tensor_tensor(cmpy, cmpy, shift.unsqueeze(1).broadcast_to([P, 2 * NT, X]), ALU.mult))
            link(v.tensor_reduce(expT[:].rearrange("p t k -> p (t k)"), cmpy, AX.X, ALU.add))
            v.sem_inc(s_tab, 1)
            link(v.tensor_tensor(posT[:], posT[:], expT[:], ALU.add))

            def copy_w(t, k, first=False):
                ex = v.value_load(expI[0:1, ds(t, 1)], min_val=0, max_val=X - 1)
                if not first:
                    v.wait_ge(f_hT, t - 1)
                v.tensor_copy(w1c[k % 2], w1s[:, ds(ex, 1), :, :].rearrange("p o c f -> p (o c) f")).then_inc(f_w, 1)

            def expert_four(i, first):
                for k in range(4):
                    t = 4 * i + k
                    v.wait_ge(f_y, t + 1)
                    v.wait_ge(s_b2in[k % 2], 32 * i + 16 * (k // 2 + 1))
                    if not (first and k < 2):
                        v.wait_ge(s_yst[k % 2], 32 * i + 16 * (k // 2))
                    v.tensor_tensor(yo[k % 2], ps_y2[k % 2], b2t[k % 2], ALU.add).then_inc(f_yo, 1)
                    copy_w(t + 3, k + 1)

            body_steps[expert_four] = 0
            v.wait_ge(s_w, 16 * 8)
            v.wait_ge(s_tail, 16 * X)
            copy_w(0, 0, first=True)
            link(v.tensor_tensor(topv[:, :, 1], topv[:, :, 1], topv[:, :, 0], ALU.subtract))
            v.sem_inc(s_ask, 1)
            v.wait_ge(s_act, NU + NT + NU + 1)
            link(v.tensor_scalar(topv[:, :, 0], topv[:, :, 1], 1.0, None, ALU.add))
            link(v.reciprocal(topv[:, :, 0], topv[:, :, 0]))
            link(v.tensor_tensor(topv[:, :, 1], topv[:, :, 1], topv[:, :, 0], ALU.mult))
            copy_w(1, 1, first=True)
            copy_w(2, 2)
            expert_four(0, True)
            loop(1, FT // 4, expert_four)

            for k in range(2):
                v.tensor_copy(idxz[k][:], posT[:, k * U:(k + 1) * U, :]).then_inc(s_idxc, 1)
            v.sem_inc(s_ask, 1)
            v.wait_ge(s_gb, 32)
            combine_front(0, 0, 0)
            combine_scales(0)
            combine_pair(0, True)
            loop(1, NU // 2 - 2, combine_pair)
            combine_pair(NU // 2 - 2, False)
            combine_pair(NU // 2 - 1, False, last=True)

        @block.tensor
        def _(pe):
            pe.sem_inc(s_msg, EB)
            pe.sem_inc(s_acc, 2)
            pe.sem_inc(s_yi, 3)
            pe.wait_ge(s_const, NCONST)
            pe.wait_ge(s_cload, NCLOAD)

            def turn_src(b, g, k):
                pe.wait_ge(s_d, EB * b + 4 * g + 4)
                for j in range(4):
                    a = pe.transpose(ps_src[:, j, :], srcb[k][:, 4 * g + j:4 * g + j + 1].broadcast_to([P, P]), ident[:])
                a.then_inc(s_tr, 1)

            def turn_next(b, k):
                pe.wait_ge(s_prep, b + 1)
                turn_src(b, 0, k)

            def message(b, q):
                pe.wait_ge(s_evac, 4 * b + q + 4)
                for j in (2 * q, 2 * q + 1):
                    pe.wait_ge(s_d, EB * b + j + 5)
                    pe.wait_ge(s_gath[j], 16 * (b + 1))
                    pe.matmul(ps_msg[:, j % 2, :], wd[j], gx[j], start=True, stop=True).then_inc(s_msg, 1)

            def moments(s, k, part_, first=False):
                started = set() if first else {0, 1, 2, 3}

                def add(b, out_, lhsT, rhs):
                    a = pe.matmul(out_, lhsT, rhs, start=b not in started, stop=False, skip_group_check=True)
                    started.add(b)
                    return a

                if part_ == 0:
                    pe.wait_ge(s_kk, s + 1)
                    pe.wait_ge(s_v1, s + 1)
                for h in ((0, 1), (2, 3, 4), (5, 6, 7))[part_]:
                    for g in range(KC):
                        c = h * KC + g
                        if first and c in (4 * 2, 4 * 5) and c // 15 == (c - 1) // 15:
                            started.add(c // 15)
                        add(c // 15, chunk_out(c), kk[k][:, h, 4 * g:4 * g + 4, :].rearrange("p s i -> p (s i)"), v1[k][:, h, :])
                if part_ == 2:
                    va = v1[k].rearrange("p h e -> p (h e)")
                    for g in range(2):
                        cols = va[:, W4 * g:W4 * (g + 1)]
                        add(2, sum_k[g], kc[k][:, g * P:(g + 1) * P], cols)
                        add(3, sum_16[g], k16[k], cols)
                        a = add(2 if g == 0 else 3, sum_v[g], ones[:], cols)
                    a.then_inc(s_acc, 1)

            def turn_xn(s, k):
                pe.wait_ge(s_xst, s + 1)
                pe.wait_ge(s_bias, s + 1)
                for c in range(2):
                    a = pe.transpose(ps_xT[:, c * P:(c + 1) * P], xst[k][:, c * P:(c + 1) * P], ident[:])
                a.then_inc(s_xTp, 1)

            def project_in(s, k):
                pe.wait_ge(s_xT, s + 1)
                for lo, hi in ((0, 512), (512, 3 * C)):
                    for c in range(2):
                        a = pe.matmul(bqk[:, lo:hi], xT[k][:, c, :], wqkv[:, c, lo:hi], start=(c == 0), stop=(c == 1))
                a.then_inc(s_qkv, 1)

            def key_turn(s, k, first=False, second=False, last=False):
                if not first:
                    moments(s - 1, 1 - k, 0, second)
                message(s, 0)
                turn_src(s, 1, k)
                if not last:
                    turn_xn(s + 1, 1 - k)
                message(s, 1)
                if not first:
                    moments(s - 1, 1 - k, 1, second)
                if not last:
                    project_in(s + 1, 1 - k)
                message(s, 2)
                if not first:
                    moments(s - 1, 1 - k, 2, second)
                turn_next(s + 1, 1 - k)
                message(s, 3)

            turn_next(0, 0)
            turn_xn(0, 0)
            project_in(0, 0)
            key_turn(0, 0, first=True)
            key_turn(1, 1, second=True)
            with pe.Fori(1, NT // 2 - 1) as i:
                for k in range(2):
                    key_turn(2 * i + k, k)
            key_turn(NT - 2, 0)
            key_turn(NT - 1, 1, last=True)
            moments(NT - 1, 1, 0)
            message(NT, 0)
            turn_src(NT, 1, 0)
            moments(NT - 1, 1, 1)
            message(NT, 1)
            moments(NT - 1, 1, 2)
            message(NT, 2)
            turn_next(NT + 1, 1)
            message(NT, 3)
            pe.wait_ge(s_mom, 1)

            def query_item(s, m, k):
                pe.wait_ge(s_qq, QI * s + m + 1)
                pe.wait_ge(s_qn, QI * s + m + 1)
                if m == 0:
                    parts = [k16[k], kc[k][:, 0:P], kc[k][:, P:2 * P]]
                else:
                    parts = [kk[k][:, m - 1, 4 * g:4 * g + 4, :].rearrange("p s i -> p (s i)") for g in range(KC)]
                for g, src in enumerate(parts):
                    a = pe.transpose(bank[m % 3][:, g * P:(g + 1) * P], src, ident[:])
                a.then_inc(s_qtr, 1)

            def sum_item(s, m, k):
                pe.wait_ge(s_qq, QI * s + m + 4)
                if m == 0:
                    pe.matmul(ps_y, qq[0][:, 0, :], m16, start=True, stop=False, skip_group_check=True)
                    for g in range(2):
                        a = pe.matmul(ps_y[:, W4 * g:W4 * (g + 1)], qq[0][:, 1 + g, :], m1[:, g, :], start=False, stop=False,
                                      skip_group_check=True)
                else:
                    h = m - 1
                    for g in range(KC):
                        a = pe.matmul(ps_y[:, VH * h:VH * (h + 1)], qq[m % 3][:, g, :], m2[:, KC * h + g, :], start=False,
                                      stop=(m == QI - 1 and g == KC - 1), skip_group_check=True)
                a.then_inc(s_yi, 1)

            def query_turn(s, k, last=False):
                b = NT + 1 + s
                for m in range(QI):
                    query_item(s, m, k)
                    if m >= 2:
                        sum_item(s, m - 2, k)
                    if m == 3 and not last:
                        message(b, 0)
                        turn_src(b, 1, 1 - k)
                    if m == 6 and not last:
                        message(b, 1)
                sum_item(s, QI - 2, k)
                sum_item(s, QI - 1, k)
                if not last:
                    message(b, 2)
                pe.wait_ge(s_on, s + 1)
                for c in range(2):
                    a = pe.transpose(ps_oT[:, c * P:(c + 1) * P], on[k][:, c * P:(c + 1) * P], ident[:])
                a.then_inc(s_oTp, 1)
                if not (isinstance(s, int) and s >= NT - 2):
                    turn_next(b + 1, k)
                if not last:
                    message(b, 3)
                pe.wait_ge(s_oT, s + 1)
                for c in range(2):
                    a = pe.matmul(ps_pr, oT[k][:, c, :], wproj[:, c, :], start=(c == 0), stop=(c == 1))
                a.then_inc(s_pr, 1)

            with pe.Fori(0, NT // 2 - 1) as i:
                for k in range(2):
                    query_turn(2 * i + k, k)
            query_turn(NT - 2, 0)
            query_turn(NT - 1, 1, last=True)

            def logits(u, k):
                def turn(j):
                    g = (U * k + j) % 2
                    pe.wait_ge(s_z, u * U + j + 1)
                    for c in range(2):
                        a = pe.transpose(ps_zT[g][:, c * P:(c + 1) * P], zt5[k][:, j, c * P:(c + 1) * P], ident[:])
                    a.then_inc(s_zTp, 1)

                turn(0)
                for j in range(U):
                    if j < U - 1:
                        turn(j + 1)
                    pe.wait_ge(s_zT, u * U + j + 1)
                    for c in range(2):
                        a = pe.matmul(ps_lg[k][:, j * X:(j + 1) * X], zT[(U * k + j) % 2][:, c, :], gw[:, c, :],
                                      start=(c == 0), stop=(c == 1))
                a.then_inc(s_lg, 1)

            def rank(u):
                pe.wait_ge(s_cc, u + 1)
                pe.matmul(ps_rk, upper[:], cc.rearrange("p u e -> p (u e)"), start=True, stop=False, skip_group_check=True)
                pe.matmul(ps_rk.rearrange("p (u e) -> p u e", u=U), ones[:], crun[:].unsqueeze(1).broadcast_to([P, U, X]),
                          start=False, stop=False, skip_group_check=True)
                for j in range(U - 1):
                    later = U - 1 - j
                    a = pe.matmul(ps_rk[:, (j + 1) * X:U * X].rearrange("p (u e) -> p u e", u=later), ones[:],
                                  cc[:, j:j + 1, :].broadcast_to([P, later, X]), start=False, stop=(j == U - 2),
                                  skip_group_check=True)
                a.then_inc(s_rk, 1)

            logits(0, 0)
            with pe.Fori(0, NU // 2 - 1) as i:
                for k in range(2):
                    rank(2 * i + k)
                    logits(2 * i + k + 1, 1 - k)
            rank(NU - 2)
            logits(NU - 1, 1)
            rank(NU - 1)
            pe.wait_ge(s_cc, NU + 1)
            pe.matmul(ps_cnt, ones[:], crun[:], start=True, stop=True).then_inc(s_cnt, 1)

            def turn_z(t, k):
                pe.transpose(ps_zT[k % 2][:, 0:P], zt[k % 4][:, 0:P], ident[:])
                pe.transpose(ps_zT[k % 2][:, P:2 * P], zt[k % 4][:, P:2 * P], ident[:]).then_inc(f_zT, 1)

            def hidden(t, k):
                pe.wait_ge(f_zTe, t + 3)
                pe.wait_ge(f_w, t + 1)
                pe.wait_ge(f_hTe, t + 1)
                for f in range(FC):
                    for c in range(2):
                        a = pe.matmul(ps_hT[k % 2][:, f * P:(f + 1) * P], w1c[k % 2][:, c, f * P:(f + 1) * P],
                                      zT[k % 2][:, c, :], start=(c == 0), stop=(c == 1))
                a.then_inc(f_hT, 1)

            pe.wait_ge(s_tab, 2)
            pe.wait_ge(s_w, 16 * 8)
            for k in range(2):
                pe.wait_ge(s_ztin[k], 16)
                turn_z(k, k)
            hidden(0, 0)
            with pe.Fori(0, FT // 4) as i:
                for k in range(4):
                    t = 4 * i + k
                    hidden(t + 1, k + 1)
                    pe.wait_ge(s_ztin[(k + 2) % 4], 16 * (i + 1 + (k + 2) // 4))
                    turn_z(t + 2, k + 2)
                    ex = pe.value_load(expI[0:1, ds(t, 1)], min_val=0, max_val=X - 1)
                    pe.wait_ge(f_hTe, t + 3)
                    pe.wait_ge(f_yo, t + 1)
                    for c in range(FC):
                        a = pe.matmul(ps_y2[k % 2], hT[k % 2][:, c, :], w2s[:, ds(ex, 1), c, :].rearrange("p o f -> p (o f)"),
                                      start=(c == 0), stop=(c == FC - 1))
                    a.then_inc(f_y, 1)


def kernel(x, src, dst, edge_weight, L0_mix_Wqkv, L0_mix_bqkv, L0_mix_Wproj, L0_mix_bproj, L0_mix_temperature,
           L0_ffn_gate_w, L0_ffn_gate_b, L0_ffn_w1, L0_ffn_b1, L0_ffn_w2, L0_ffn_b2, L0_ffn_gamma, L0_ffn_beta):
    import numpy as np
    import concourse.bacc as bacc
    from concourse.bass_utils import run_bass_kernel_spmd

    def edges(a):
        a = np.asarray(a)
        full = np.zeros(((NB + 1) * EB * P,), a.dtype)
        full[:E] = a
        return np.ascontiguousarray(full.reshape(-1, P).T)

    xp = np.zeros((NP, C), np.float32)
    xp[:N] = np.asarray(x)
    arrays = {
        "x_pad": xp, "src_t": edges(src), "dst_t": edges(dst), "w_t": edges(edge_weight),
        "wqkv_t": np.ascontiguousarray(np.asarray(L0_mix_Wqkv).T), "bqkv": np.asarray(L0_mix_bqkv),
        "wproj_t": np.ascontiguousarray(np.asarray(L0_mix_Wproj).T), "bproj": np.asarray(L0_mix_bproj),
        "temperature": np.asarray(L0_mix_temperature).reshape(H),
        "gate_w": np.asarray(L0_ffn_gate_w), "gate_b": np.asarray(L0_ffn_gate_b), "w1": np.asarray(L0_ffn_w1),
        "b1_t": np.ascontiguousarray(np.asarray(L0_ffn_b1).reshape(X, FC, P).transpose(2, 0, 1).reshape(P, X * FC)),
        "w2": np.asarray(L0_ffn_w2), "b2": np.asarray(L0_ffn_b2), "gamma": np.asarray(L0_ffn_gamma),
        "beta": np.asarray(L0_ffn_beta),
    }
    nc = bacc.Bacc("TRN2", target_bir_lowering=False, num_devices=1)
    args = [nc.dram_tensor(k, a.shape, mybir.dt.from_np(a.dtype), kind="ExternalInput").ap() for k, a in arrays.items()]
    args.append(nc.dram_tensor("y_out", (NP, C), F32, kind="ExternalOutput").ap())
    program(nc, *args)
    r = run_bass_kernel_spmd(nc, [arrays], core_ids=[0])
    return r.results[0]["y_out"][:N]
```
